# Optimizing a Trainium2 kernel written in Bass

```python
import numpy as np
import jax
import jax.numpy as jnp

def _softmax(x, axis=-1):
    return jax.nn.softmax(x, axis=axis)

def _gelu(x):
    return jax.nn.gelu(x, approximate=True)

def _silu(x):
    return jax.nn.silu(x)

def _sigmoid(x):
    return jax.nn.sigmoid(x)

def _layernorm(x, axis=-1, eps=1e-05):
    m = jnp.mean(x, axis=axis, keepdims=True)
    v = jnp.var(x, axis=axis, keepdims=True)
    return (x - m) / jnp.sqrt(v + eps)

def _scatter_add(tgt, idx, src, axis=0):
    return tgt.at[idx].add(src)

def _segment_sum(src, seg, n):
    return jax.ops.segment_sum(src, seg, n)
kernel_name = 'mk_hybrid_d1_jaxref_r8_ffb089'

def setup_inputs(seed: int=0):
    np.random.seed(seed)
    _w = jnp.asarray

    def _L0_attn_a_setup():
        import jax, jax.numpy as jnp
        import numpy as np
        DEPTH, DIM, H, DH, MKV, TOPK = (2, 128, 16, 64, 32, 64)
        INNER = H * DH
        FFD = 4 * DIM
        SCALE = DH ** (-0.5)
        EPS = 1e-05

        def layer_norm(x, g, b):
            mu = x.mean(-1, keepdims=True)
            var = ((x - mu) ** 2).mean(-1, keepdims=True)
            return (x - mu) * jax.lax.rsqrt(var + EPS) * g + b

        def attn_block(x, wq, wk, wv, mk, mv, pre, post, wo, bo):
            b, n, _ = x.shape
            q = (x @ wq).reshape(b, n, H, DH).transpose(0, 2, 1, 3)
            k = (x @ wk).reshape(b, n, H, DH).transpose(0, 2, 1, 3)
            v = (x @ wv).reshape(b, n, H, DH).transpose(0, 2, 1, 3)
            mk_b = jnp.broadcast_to(mk[None], (b, H, MKV, DH))
            mv_b = jnp.broadcast_to(mv[None], (b, H, MKV, DH))
            k = jnp.concatenate([mk_b, k], axis=2)
            v = jnp.concatenate([mv_b, v], axis=2)
            dots = jnp.einsum('bhid,bhjd->bhij', q, k) * SCALE
            dots = jnp.einsum('bhij,hk->bkij', dots, pre)
            neg = -jnp.finfo(dots.dtype).max
            j = n + MKV
            causal = jnp.arange(n)[:, None] + MKV < jnp.arange(j)[None, :]
            dots = jnp.where(causal[None, None], neg, dots)
            vk = jax.lax.top_k(dots, TOPK)[0][..., -1:]
            dots = jnp.where(dots < vk, neg, dots)
            attn = jax.nn.softmax(dots, axis=-1)
            attn = jnp.einsum('bhij,hk->bkij', attn, post)
            out = jnp.einsum('bhij,bhjd->bhid', attn, v)
            out = out.transpose(0, 2, 1, 3).reshape(b, n, INNER)
            return out @ wo + bo

        def ff_block(x, w1, b1, w2, b2):
            return jax.nn.gelu(x @ w1 + b1, approximate=False) @ w2 + b2
        key = jax.random.key(seed)
        ks = jax.random.split(key, 16)
        s = 0.02
        inp = {'x': jax.random.normal(ks[0], (4, 128, DIM), jnp.float32), 'ln1_g': jnp.ones((DEPTH, DIM), jnp.float32), 'ln1_b': jnp.zeros((DEPTH, DIM), jnp.float32), 'wq': jax.random.normal(ks[1], (DEPTH, DIM, INNER), jnp.float32) * s, 'wk': jax.random.normal(ks[2], (DEPTH, DIM, INNER), jnp.float32) * s, 'wv': jax.random.normal(ks[3], (DEPTH, DIM, INNER), jnp.float32) * s, 'mem_k': jax.random.normal(ks[4], (DEPTH, H, MKV, DH), jnp.float32), 'mem_v': jax.random.normal(ks[5], (DEPTH, H, MKV, DH), jnp.float32), 'pre_proj': jax.random.normal(ks[6], (DEPTH, H, H), jnp.float32), 'post_proj': jax.random.normal(ks[7], (DEPTH, H, H), jnp.float32), 'wo': jax.random.normal(ks[8], (DEPTH, INNER, DIM), jnp.float32) * s, 'bo': jnp.zeros((DEPTH, DIM), jnp.float32), 'ln2_g': jnp.ones((DEPTH, DIM), jnp.float32), 'ln2_b': jnp.zeros((DEPTH, DIM), jnp.float32), 'w1': jax.random.normal(ks[9], (DEPTH, DIM, FFD), jnp.float32) * s, 'b1': jnp.zeros((DEPTH, FFD), jnp.float32), 'w2': jax.random.normal(ks[10], (DEPTH, FFD, DIM), jnp.float32) * s, 'b2': jnp.zeros((DEPTH, DIM), jnp.float32)}
        return inp
    _L0_attn_a_in = _L0_attn_a_setup()

    def _L0_attn_b_setup():
        import jax, jax.numpy as jnp
        import numpy as np
        N_HEADS = 16

        def _heads(x, h):
            B, T, D = x.shape
            return x.reshape(B, T, h, D // h).transpose(0, 2, 1, 3)

        def _reference_tuple_inner(x, Wq, Wk, Wv, Wo, Wg, bg):
            h = N_HEADS
            q = _heads(x @ Wq.T, h)
            k = _heads(x @ Wk.T, h)
            v = _heads(x @ Wv.T, h)
            g = _heads(jax.nn.sigmoid(x @ Wg.T + bg), h)
            qf = jax.nn.softplus(q) * (g + 1e-06)
            kf = jax.nn.softplus(k)
            kv = kf[..., :, None] * v[..., None, :]
            kv_cum = jnp.cumsum(kv, axis=2)
            z_cum = jnp.cumsum(kf, axis=2)
            num = jnp.einsum('bhtd,bhtde->bhte', qf, kv_cum)
            den = jnp.einsum('bhtd,bhtd->bht', qf, z_cum) + 1e-06
            out = num / den[..., None]
            B, _, T, dh = out.shape
            out = out.transpose(0, 2, 1, 3).reshape(B, T, h * dh)
            out = out @ Wo.T
            return (out, kv_cum[:, :, -1], z_cum[:, :, -1])
        key = jax.random.key(seed)
        B, T, D = (1, 256, 128)
        ks = jax.random.split(key, 7)
        s = 0.02
        return {'x': jax.random.normal(ks[0], (B, T, D), jnp.float32), 'Wq': jax.random.normal(ks[1], (D, D), jnp.float32) * s, 'Wk': jax.random.normal(ks[2], (D, D), jnp.float32) * s, 'Wv': jax.random.normal(ks[3], (D, D), jnp.float32) * s, 'Wo': jax.random.normal(ks[4], (D, D), jnp.float32) * s, 'Wg': jax.random.normal(ks[5], (D, D), jnp.float32) * s, 'bg': jax.random.normal(ks[6], (D,), jnp.float32) * s}
    _L0_attn_b_in = _L0_attn_b_setup()

    def _L0_ffn_setup():
        import jax, jax.numpy as jnp
        import numpy as np
        DIM = 128
        NUM_EXPERTS = 8
        HIDDEN = 512
        CAP_FACTOR = 2.0
        B, S = (4, 256)
        key = jax.random.key(seed)
        ks = jax.random.split(key, 6)
        scale_r = 1.0 / np.sqrt(DIM)
        scale_1 = 1.0 / np.sqrt(DIM)
        scale_2 = 1.0 / np.sqrt(HIDDEN)
        return {'x': jax.random.normal(ks[0], (B, S, DIM), dtype=jnp.float32), 'router_w': jax.random.uniform(ks[1], (NUM_EXPERTS, DIM), jnp.float32, -scale_r, scale_r), 'w1': jax.random.uniform(ks[2], (NUM_EXPERTS, DIM, HIDDEN), jnp.float32, -scale_1, scale_1), 'b1': jax.random.uniform(ks[3], (NUM_EXPERTS, HIDDEN), jnp.float32, -scale_1, scale_1), 'w2': jax.random.uniform(ks[4], (NUM_EXPERTS, HIDDEN, DIM), jnp.float32, -scale_2, scale_2), 'b2': jax.random.uniform(ks[5], (NUM_EXPERTS, DIM), jnp.float32, -scale_2, scale_2)}
    _L0_ffn_in = _L0_ffn_setup()
    _d = {'L0_attn_a_x': _L0_attn_a_in['x'], 'L0_attn_a_ln1_g': _L0_attn_a_in['ln1_g'], 'L0_attn_a_ln1_b': _L0_attn_a_in['ln1_b'], 'L0_attn_a_wq': _L0_attn_a_in['wq'], 'L0_attn_a_wk': _L0_attn_a_in['wk'], 'L0_attn_a_wv': _L0_attn_a_in['wv'], 'L0_attn_a_mem_k': _L0_attn_a_in['mem_k'], 'L0_attn_a_mem_v': _L0_attn_a_in['mem_v'], 'L0_attn_a_pre_proj': _L0_attn_a_in['pre_proj'], 'L0_attn_a_post_proj': _L0_attn_a_in['post_proj'], 'L0_attn_a_wo': _L0_attn_a_in['wo'], 'L0_attn_a_bo': _L0_attn_a_in['bo'], 'L0_attn_a_ln2_g': _L0_attn_a_in['ln2_g'], 'L0_attn_a_ln2_b': _L0_attn_a_in['ln2_b'], 'L0_attn_a_w1': _L0_attn_a_in['w1'], 'L0_attn_a_b1': _L0_attn_a_in['b1'], 'L0_attn_a_w2': _L0_attn_a_in['w2'], 'L0_attn_a_b2': _L0_attn_a_in['b2'], 'L0_attn_b_Wq': _L0_attn_b_in['Wq'], 'L0_attn_b_Wk': _L0_attn_b_in['Wk'], 'L0_attn_b_Wv': _L0_attn_b_in['Wv'], 'L0_attn_b_Wo': _L0_attn_b_in['Wo'], 'L0_attn_b_Wg': _L0_attn_b_in['Wg'], 'L0_attn_b_bg': _L0_attn_b_in['bg'], 'L0_ffn_router_w': _L0_ffn_in['router_w'], 'L0_ffn_w1': _L0_ffn_in['w1'], 'L0_ffn_b1': _L0_ffn_in['b1'], 'L0_ffn_w2': _L0_ffn_in['w2'], 'L0_ffn_b2': _L0_ffn_in['b2']}
    _x0 = _d['L0_attn_a_x']
    _d['L0_attn_a_x'] = jax.random.normal(jax.random.fold_in(jax.random.key(seed), 1), (16, 256, 128), dtype=_x0.dtype)
    del _x0
    return _d

def reference(L0_attn_a_x, L0_attn_a_ln1_g, L0_attn_a_ln1_b, L0_attn_a_wq, L0_attn_a_wk, L0_attn_a_wv, L0_attn_a_mem_k, L0_attn_a_mem_v, L0_attn_a_pre_proj, L0_attn_a_post_proj, L0_attn_a_wo, L0_attn_a_bo, L0_attn_a_ln2_g, L0_attn_a_ln2_b, L0_attn_a_w1, L0_attn_a_b1, L0_attn_a_w2, L0_attn_a_b2, L0_attn_b_Wq, L0_attn_b_Wk, L0_attn_b_Wv, L0_attn_b_Wo, L0_attn_b_Wg, L0_attn_b_bg, L0_ffn_router_w, L0_ffn_w1, L0_ffn_b1, L0_ffn_w2, L0_ffn_b2):

    def _L0_attn_a_ref(x, ln1_g, ln1_b, wq, wk, wv, mem_k, mem_v, pre_proj, post_proj, wo, bo, ln2_g, ln2_b, w1, b1, w2, b2):
        import jax, jax.numpy as jnp
        import numpy as np
        DEPTH, DIM, H, DH, MKV, TOPK = (2, 128, 16, 64, 32, 64)
        INNER = H * DH
        FFD = 4 * DIM
        SCALE = DH ** (-0.5)
        EPS = 1e-05

        def layer_norm(x, g, b):
            mu = x.mean(-1, keepdims=True)
            var = ((x - mu) ** 2).mean(-1, keepdims=True)
            return (x - mu) * jax.lax.rsqrt(var + EPS) * g + b

        def attn_block(x, wq, wk, wv, mk, mv, pre, post, wo, bo):
            b, n, _ = x.shape
            q = (x @ wq).reshape(b, n, H, DH).transpose(0, 2, 1, 3)
            k = (x @ wk).reshape(b, n, H, DH).transpose(0, 2, 1, 3)
            v = (x @ wv).reshape(b, n, H, DH).transpose(0, 2, 1, 3)
            mk_b = jnp.broadcast_to(mk[None], (b, H, MKV, DH))
            mv_b = jnp.broadcast_to(mv[None], (b, H, MKV, DH))
            k = jnp.concatenate([mk_b, k], axis=2)
            v = jnp.concatenate([mv_b, v], axis=2)
            dots = jnp.einsum('bhid,bhjd->bhij', q, k) * SCALE
            dots = jnp.einsum('bhij,hk->bkij', dots, pre)
            neg = -jnp.finfo(dots.dtype).max
            j = n + MKV
            causal = jnp.arange(n)[:, None] + MKV < jnp.arange(j)[None, :]
            dots = jnp.where(causal[None, None], neg, dots)
            vk = jax.lax.top_k(dots, TOPK)[0][..., -1:]
            dots = jnp.where(dots < vk, neg, dots)
            attn = jax.nn.softmax(dots, axis=-1)
            attn = jnp.einsum('bhij,hk->bkij', attn, post)
            out = jnp.einsum('bhij,bhjd->bhid', attn, v)
            out = out.transpose(0, 2, 1, 3).reshape(b, n, INNER)
            return out @ wo + bo

        def ff_block(x, w1, b1, w2, b2):
            return jax.nn.gelu(x @ w1 + b1, approximate=False) @ w2 + b2
        for l in range(DEPTH):
            a = attn_block(layer_norm(x, ln1_g[l], ln1_b[l]), wq[l], wk[l], wv[l], mem_k[l], mem_v[l], pre_proj[l], post_proj[l], wo[l], bo[l])
            x = a + x
            f = ff_block(layer_norm(x, ln2_g[l], ln2_b[l]), w1[l], b1[l], w2[l], b2[l])
            x = f + x
        return x

    def _L0_attn_b_ref(x, Wq, Wk, Wv, Wo, Wg, bg):
        import jax, jax.numpy as jnp
        import numpy as np
        N_HEADS = 16

        def _heads(x, h):
            B, T, D = x.shape
            return x.reshape(B, T, h, D // h).transpose(0, 2, 1, 3)

        def _reference_tuple_inner(x, Wq, Wk, Wv, Wo, Wg, bg):
            h = N_HEADS
            q = _heads(x @ Wq.T, h)
            k = _heads(x @ Wk.T, h)
            v = _heads(x @ Wv.T, h)
            g = _heads(jax.nn.sigmoid(x @ Wg.T + bg), h)
            qf = jax.nn.softplus(q) * (g + 1e-06)
            kf = jax.nn.softplus(k)
            kv = kf[..., :, None] * v[..., None, :]
            kv_cum = jnp.cumsum(kv, axis=2)
            z_cum = jnp.cumsum(kf, axis=2)
            num = jnp.einsum('bhtd,bhtde->bhte', qf, kv_cum)
            den = jnp.einsum('bhtd,bhtd->bht', qf, z_cum) + 1e-06
            out = num / den[..., None]
            B, _, T, dh = out.shape
            out = out.transpose(0, 2, 1, 3).reshape(B, T, h * dh)
            out = out @ Wo.T
            return (out, kv_cum[:, :, -1], z_cum[:, :, -1])
        return _reference_tuple_inner(x, Wq, Wk, Wv, Wo, Wg, bg)[0]

    def _L0_ffn_ref(x, router_w, w1, b1, w2, b2):
        import jax, jax.numpy as jnp
        import numpy as np
        DIM = 128
        NUM_EXPERTS = 8
        HIDDEN = 512
        CAP_FACTOR = 2.0
        B, S = (4, 256)
        Bz, Sz, Dz = x.shape
        E = router_w.shape[0]
        capacity = max(1, int(Sz * CAP_FACTOR / E) + 1)
        scores = jax.nn.softmax(jnp.einsum('bsd,ed->bse', x, router_w), axis=-1)
        scores_t = jnp.swapaxes(scores, 1, 2)
        gate_vals, sel_idx = jax.lax.top_k(scores_t, capacity)
        b_idx = jnp.arange(Bz)[:, None, None]
        tokens = x[b_idx, sel_idx]
        h = jnp.einsum('becd,edh->bech', tokens, w1) + b1[None, :, None, :]
        h = jax.nn.gelu(h, approximate=False)
        y = jnp.einsum('bech,ehd->becd', h, w2) + b2[None, :, None, :]
        gated = y * gate_vals[..., None]
        out = jnp.zeros_like(x).at[b_idx, sel_idx].add(gated)
        return out
    x = L0_attn_a_x
    x = x + _L0_attn_a_ref(_layernorm(x, axis=-1), L0_attn_a_ln1_g, L0_attn_a_ln1_b, L0_attn_a_wq, L0_attn_a_wk, L0_attn_a_wv, L0_attn_a_mem_k, L0_attn_a_mem_v, L0_attn_a_pre_proj, L0_attn_a_post_proj, L0_attn_a_wo, L0_attn_a_bo, L0_attn_a_ln2_g, L0_attn_a_ln2_b, L0_attn_a_w1, L0_attn_a_b1, L0_attn_a_w2, L0_attn_a_b2)
    x = x + _L0_ffn_ref(_layernorm(x, axis=-1), L0_ffn_router_w, L0_ffn_w1, L0_ffn_b1, L0_ffn_w2, L0_ffn_b2)
    x = x + _L0_attn_b_ref(_layernorm(x, axis=-1), L0_attn_b_Wq, L0_attn_b_Wk, L0_attn_b_Wv, L0_attn_b_Wo, L0_attn_b_Wg, L0_attn_b_bg)
    x = x + _L0_ffn_ref(_layernorm(x, axis=-1), L0_ffn_router_w, L0_ffn_w1, L0_ffn_b1, L0_ffn_w2, L0_ffn_b2)
    return x

_drawn_inputs = setup_inputs


def setup_inputs(seed=0):
    import zlib

    import numpy as np

    out = dict(_drawn_inputs(seed))
    spreads = {'L0_attn_a_ln1_g': (1.0, 0.2),
     'L0_attn_a_ln1_b': (0.0, 0.1),
     'L0_attn_a_bo': (0.0, 0.1),
     'L0_attn_a_ln2_g': (1.0, 0.6),
     'L0_attn_a_ln2_b': (0.0, 0.8),
     'L0_attn_a_b1': (0.0, 0.401),
     'L0_attn_a_b2': (0.0, 0.1)}
    factors = {'L0_attn_b_Wq': 8.0,
     'L0_attn_b_Wk': 8.0,
     'L0_attn_b_Wv': 8.0,
     'L0_attn_b_Wo': 8.0,
     'L0_attn_b_Wg': 8.0,
     'L0_attn_b_bg': 64.0,
     'L0_ffn_b1': 8.0,
     'L0_ffn_b2': 6.902}
    for name, (base, spread) in spreads.items():
        noise = np.random.default_rng([zlib.crc32(name.encode()), seed]).standard_normal(out[name].shape)
        drawn = base * np.exp(spread * noise) if base else spread * noise
        out[name] = jnp.asarray(drawn.astype(out[name].dtype))
    for name, factor in factors.items():
        out[name] = (out[name] * factor).astype(out[name].dtype)
    return out
```

```python
from contextlib import ExitStack

import concourse.bass as bass
from concourse import mybir

ALU = mybir.AluOpType
ACT = mybir.ActivationFunctionType
F32 = mybir.dt.float32

P = 128
B, T, D = 16, 256, 128
TT = T // P
H, DH, MKV, TOPK = 16, 64, 32, 64
DEPTH = 2
NC_H = H * DH // P
J = MKV + T
FC = 4 * D // P
ROWS = P // H
TILES = T // ROWS
HALF = TILES // TT
STEPS = 4
WI = [MKV + P, J]
EPS = 1e-5
MASKED = -(2.0 ** 126)
TAKEN = -3.0e38
DR, XS, ES = 4, 4, 4


def width(t):
    return ROWS * (t + 1) + MKV


def key_chunks(w):
    return [(j, min(P, w - j)) for j in range(0, w, P)]


class Turns:

    def __init__(self, names, banks):
        self.at = {name: n for n, name in enumerate(names)}
        self.banks = banks

    def bank(self, name):
        return self.at[name] % self.banks

    def full(self, name):
        return self.at[name] // self.banks + 1

    def free(self, name):
        return self.at[name] // self.banks


def wait(eng, sem, value):
    if value > 0:
        eng.wait_ge(sem, value)


def side_plan():
    plan = {t: [] for t in range(TILES)}
    for n in range(4):
        plan[2 + n].append(("av1", n))
    for h in range(H):
        plan[6 + h // 4].append(("dots1", h))
    plan[9].append(("wo1", 0))
    plan[12].append(("turn_ff", 0))
    plan[14] += [("up", 0), ("up", 1)]
    plan[16].append(("down", 0))
    for n in range(4):
        plan[18 + n].append(("av0", n))
    plan[22] += [("wo0", 0), ("turn_qkv", 0)]
    for c in range(NC_H):
        plan[24 + c // 4].append(("qk", c))
    for h in range(H):
        plan[26 + h // 8].append(("dots0", h))
    for n in range(6):
        plan[28 + n // 2].append(("v", n))
    return plan


ADD_WO1, BRING, ADD_DOWN, STATS_QKV, KMEM, ADD_WO0 = 10, 14, 18, 20, 22, 26
PLAN = side_plan()
FIRST_JOBS = [("turn_qkv", 0)] + [("qk", c) for c in range(NC_H)] + [("dots0", h) for h in range(H)] \
    + [("v", n) for n in range(6)]
LAST_JOBS = [("av1", n) for n in range(4)] + [("wo1", 0), ("turn_ff", 0), ("up", 0), ("up", 1), ("down", 0)]
SIDE_BANKS = 4


def takes_bank(job):
    return not (job[0] in ("av0", "av1") and job[1] % 2)


def side_turns(jobs_of_steps):
    return Turns([(s,) + job for s, jobs in jobs_of_steps for job in jobs if takes_bank(job)], SIDE_BANKS)


def program(nc, a, out):
    with ExitStack() as ctx:
        def sb(name, shape, where=None):
            return (where or ctx).enter_context(nc.sbuf_tensor(name, shape, F32))

        def sem(name):
            return ctx.enter_context(nc.semaphore(name))

        x = sb("x", [P, B + 2, TT * D])
        ident = sb("ident", [P, P])
        minus_half = sb("minus_half", [P, TT])
        ones = sb("ones", [1, P])
        mv = sb("mv", [P, 2, TT, 2])
        bst = sb("bst", [P, TT, 6])
        rstd = sb("rstd", [P, 2, TT])
        shift = sb("shift", [P, 2, TT])
        vare = sb("vare", [P, TT])

        s_load = sem("s_load")
        s_set = sem("s_set")
        s_diag = sem("s_diag")
        s_out = sem("s_out")
        s_tail = sem("s_tail")
        s_mask = sem("s_mask")
        banks = [ctx.enter_context(nc.psum_tensor(f"bank{i}", [P, 512], F32)) for i in range(8)]

        attention(nc, a, x, ident, minus_half, ones, mv, bst, rstd, shift, vare, banks, s_load, s_set, s_diag)

        tail(nc, a, x, ident, minus_half, mv, bst, rstd, vare, banks, s_tail, s_mask)
        with nc.Block() as block:
            @block.sync
            def _(sp):
                sp.dma_start(out.rearrange("b (t p) d -> p b t d", p=P),
                             x[:, 1:B + 1, :].rearrange("p b (t d) -> p b t d", t=TT)).then_inc(s_out, 16)
                sp.wait_ge(s_out, 16)


def attention(nc, a, x, ident, minus_half, ones, mv, bst, rstd, shift, vare, banks, s_load, s_set, s_diag):
    with ExitStack() as ctx:
        def sb(name, shape):
            return ctx.enter_context(nc.sbuf_tensor(name, shape, F32))

        sems = []

        def sem(name):
            s = ctx.enter_context(nc.semaphore(name))
            sems.append(s)
            return s

        wq = sb("wq", [P, DEPTH, H * DH])
        wk = sb("wk", [P, DEPTH, H * DH])
        wv = sb("wv", [P, DEPTH, H * DH])
        wo = sb("wo", [P, DEPTH, NC_H, D])
        w1 = sb("w1", [P, DEPTH, FC * P])
        w2 = sb("w2", [P, DEPTH, FC, D])
        gains = sb("gains", [P, 4, DEPTH])
        b1 = sb("b1", [P, DEPTH, FC])
        bo = sb("bo", [1, DEPTH, D])
        b2 = sb("b2", [1, DEPTH, D])
        pre = sb("pre", [P, DEPTH, P])
        post = sb("post", [P, DEPTH, H * ROWS])
        own = sb("own", [P, ROWS])
        stack = sb("stack", [P, 2, DEPTH, H])
        causal = sb("causal", [P, ROWS])

        z = sb("z", [P, 2, TT * D])
        xh = sb("xh", [P, TT * D])
        xnT = sb("xnT", [P, MKV + T])
        qT = sb("qT", [P, NC_H, T])
        kmem = sb("kmem", [P, DEPTH, NC_H, MKV])
        kT = sb("kT", [P, NC_H, J])
        v = sb("v", [P, 2, 3, H * DH])
        dots = [sb(f"dots{i}", [P, H, WI[i]]) for i in range(TT)]
        gathered = sb("gathered", [P, DR, J])
        mixed = sb("mixed", [P, XS, J])
        left = sb("left", [P, 2, J])
        top = sb("top", [P, XS, TOPK])
        nmax = sb("nmax", [P, XS])
        e = sb("e", [P, ES, J])
        total = sb("total", [P, 2])
        rtotal = sb("rtotal", [P, 2])
        spost = sb("spost", [P, 2, H * ROWS])
        pT = [[sb(f"pT{i}{c}", [n, H, P]) for c, (_, n) in enumerate(key_chunks(WI[i]))] for i in range(TT)]
        oT = sb("oT", [P, NC_H, P])
        gT = sb("gT", [P, FC, T])

        mix_bank, post_bank, side_bank = banks[0:2], banks[2:4], banks[4:8]

        with nc.Block() as block:
            @block.sync
            def _(sp):
                loads = [
                    (x[:, 1:3, :].rearrange("p b (t d) -> p b t d", t=TT),
                     a["x"][0:2].rearrange("b (t p) d -> p b t d", p=P)),
                    (x[:, 3:B + 1, :].rearrange("p b (t d) -> p b t d", t=TT),
                     a["x"][2:B].rearrange("b (t p) d -> p b t d", p=P)),
                    (wq[:, :, :], a["wq"].rearrange("l p n -> p l n")),
                    (wk[:, :, :], a["wk"].rearrange("l p n -> p l n")),
                    (wv[:, :, :], a["wv"].rearrange("l p n -> p l n")),
                    (gains[:, :, :], a["gains"]),
                    (b1[:, :, :], a["b1"]),
                    (bo[:, :, :], a["bo"][None, :, :]),
                    (b2[:, :, :], a["b2"][None, :, :]),
                ]
                for l in range(DEPTH):
                    loads.append((wo[:, l, :, :], a["wo"][l].rearrange("(c p) n -> p c n", p=P)))
                    loads.append((w2[:, l, :, :], a["w2"][l].rearrange("(c p) n -> p c n", p=P)))
                    loads.append((w1[:, l, :], a["w1"][l]))
                    for hh in range(2):
                        loads.append((kmem[hh * DH:(hh + 1) * DH, l, :, :],
                                      a["mem_kT"][l].rearrange("(c hh) d m -> hh d c m", hh=2)[hh]))
                for to, source in loads:
                    sp.dma_start(to, source).then_inc(s_load, 16)
                for n, name in enumerate(("pre", "post")):
                    for i in range(ROWS):
                        sp.dma_start(stack[i * H:(i + 1) * H, n, :, :], a[name].rearrange("l h k -> h l k")) \
                          .then_inc(s_diag, 16)
                sp.wait_ge(s_load, 16 * len(loads))
                sp.wait_ge(s_diag, 16 * 2 * ROWS)

            @block.gpsimd
            def _(pool):
                pool.memset(ident[:, :], 0.0).then_inc(s_set, 1)
                pool.memset(own[:, :], 1.0).then_inc(s_set, 1)
                pool.memset(causal[:, :], 0.0).then_inc(s_set, 1)
                pool.memset(ones[:, :], 1.0).then_inc(s_set, 1)
                pool.memset(minus_half[:, :], -0.5).then_inc(s_set, 1)
                pool.wait_ge(s_set, 3)
                pool.affine_select(out=ident[:, :], in_=ident[:, :], compare_op=ALU.not_equal, fill=1.0, base=0,
                                   pattern=[[-1, P]], channel_multiplier=1).then_inc(s_set, 1)
                pool.affine_select(out=causal[:, :], in_=causal[:, :], compare_op=ALU.is_ge, fill=MASKED, base=0,
                                   pattern=[[-H, ROWS]], channel_multiplier=1).then_inc(s_set, 1)
                pool.affine_select(out=own[:, :], in_=own[:, :], compare_op=ALU.is_ge, fill=0.0, base=0,
                                   pattern=[[-H, ROWS]], channel_multiplier=1).then_inc(s_set, 1)
                pool.wait_ge(s_set, 8)
                pool.affine_select(out=own[:, :], in_=own[:, :], compare_op=ALU.is_ge, fill=0.0, base=H - 1,
                                   pattern=[[H, ROWS]], channel_multiplier=-1).then_inc(s_set, 1)

            @block.vector
            def _(dve):
                for buf in (z[:, :, :], xnT[:, 0:MKV], x[:, 0, :], x[:, B + 1, :], v[:, :, :, :]):
                    dve.memset(buf, 0.0)
                for half in pT:
                    for chunk in half:
                        dve.memset(chunk[:, :, :], 0.0)
                dve.wait_ge(s_set, 9)
                dve.wait_ge(s_diag, 16 * 2 * ROWS)
                for l in range(DEPTH):
                    dve.tensor_tensor(pre[:, l, :].rearrange("p (i k) -> p i k", i=ROWS),
                                      stack[:, 0, l, None, :].broadcast_to([P, ROWS, H]),
                                      own[:, :, None].broadcast_to([P, ROWS, H]), ALU.mult)
                    dve.tensor_tensor(post[:, l, :].rearrange("p (k i) -> p k i", i=ROWS),
                                      stack[:, 1, l, :, None].broadcast_to([P, H, ROWS]),
                                      own[:, None, :].broadcast_to([P, H, ROWS]), ALU.mult)

        s_gath = [sem(f"s_gath{i}") for i in range(DR)]
        s_vmem = sem("s_vmem")
        s_kmem = sem("s_kmem")
        s_mix = sem("s_mix")
        s_x = sem("s_x")
        s_masked = sem("s_masked")
        s_max = sem("s_max")
        s_dve = sem("s_dve")
        s_nmax = sem("s_nmax")
        s_e = sem("s_e")
        s_r = sem("s_r")
        s_spost = sem("s_spost")
        s_post = sem("s_post")
        s_p = sem("s_p")
        s_full = [sem(f"s_full{i}") for i in range(SIDE_BANKS)]
        s_free = [sem(f"s_free{i}") for i in range(SIDE_BANKS)]
        s_xin = sem("s_xin")
        s_stats = sem("s_stats")
        s_pool = sem("s_pool")
        s_norm = sem("s_norm")

        def run(jobs_of_steps, ln_order, tiles, x_done, x_new):
            turns = Turns([(s,) + job for s, jobs in jobs_of_steps for job in jobs if takes_bank(job)], SIDE_BANKS)
            now = {s: (s % STEPS) // 2 for s, _ in jobs_of_steps}
            done = {s: ((s - 1) % STEPS) // 2 for s, _ in jobs_of_steps}
            coming = {s: ((s + 1) % STEPS) // 2 for s, _ in jobs_of_steps}

            def acquire(pe, s, job):
                b = turns.bank((s,) + job)
                wait(pe, s_free[b], turns.free((s,) + job))
                return side_bank[b], s_full[b]

            def filled(eng, s, job):
                b = turns.bank((s,) + job)
                eng.wait_ge(s_full[b], turns.full((s,) + job))
                return side_bank[b], s_free[b]

            def emptied(eng, s, job):
                if (s,) + job in turns.at:
                    eng.wait_ge(s_free[turns.bank((s,) + job)], turns.full((s,) + job))

            def vmems(s):
                return sum(1 for r, jobs in jobs_of_steps if ("v", 5) in jobs and r <= s)

            kmems = vmems

            def pool_kmem(pool, s):
                if (s, "dots1", H - 1) in turns.at:
                    filled(pool, s, ("dots1", H - 1))
                pool.tensor_copy(kT[:, :, 0:MKV], kmem[:, coming[s], :, :]).then_inc(s_kmem, 1)

            def sp_vmem(sp, s):
                emptied(sp, s, ("v", 1))
                sp.dma_start(v[0:MKV, (s + 1) % 2, 0, :].rearrange("m (h d) -> m h d", h=H),
                             a["mem_v"][coming[s]].rearrange("h m d -> m h d")).then_inc(s_vmem, 16)

            def norms(s, kind):
                return ln_order.index((s, kind)) + 1

            def pe_dots(pe, s, half, h):
                bank, full = acquire(pe, s, (f"dots{half}", h))
                if h == 0:
                    emptied(pe, s if half == 0 else s - 1, ("qk", NC_H - 1))
                    wait(pe, s_kmem, kmems(s if half == 0 else s - 1))
                lo = DH * (h % 2)
                nc.tensor.matmul(bank[:, 0:WI[half]], qT[lo:lo + DH, h // 2, half * P:(half + 1) * P],
                                 kT[lo:lo + DH, h // 2, 0:WI[half]], start=True, stop=True).then_inc(full, 1)

            def pe_av(pe, s, half, n, stream):
                if n % 2 == 0:
                    acquire(pe, s, (f"av{half}", n))
                b = turns.bank((s, f"av{half}", n - n % 2))
                if n == 0 and tiles:
                    wait(pe, s_p, TILES * s + (HALF if half == 0 else 0))
                if n == 0 and half == 0:
                    emptied(pe, s - 1, ("v", 5))
                    wait(pe, s_vmem, 16 * vmems(s - 1))
                parts = key_chunks(WI[half])
                for pair in range(2 * n, 2 * n + 2):
                    c = pair % 4
                    for k, (j, m) in enumerate(parts):
                        for lo in (0, DH):
                            h = 2 * pair + lo // DH
                            last = nc.tensor.matmul(side_bank[b][lo:lo + DH, c * P:(c + 1) * P],
                                                    v[0:m, stream, k, h * DH:(h + 1) * DH], pT[half][k][0:m, h, :],
                                                    start=(k == 0), stop=(k == len(parts) - 1))
                if n % 2 == 1:
                    last.then_inc(s_full[b], 1)

            def pe_wo(pe, s, half, layer):
                bank, full = acquire(pe, s, (f"wo{half}", 0))
                emptied(pe, s, (f"av{half}", 2))
                for c in range(NC_H):
                    nc.tensor.matmul(bank[:, 0:D], oT[:, c, :], wo[:, layer, c, :], start=(c == 0), stop=False)
                nc.tensor.matmul(bank[:, 0:D], ones[0:1, :], bo[0:1, layer, :], start=False, stop=True) \
                    .then_inc(full, 1)

            def pe_turn(pe, s, name, kind):
                bank, full = acquire(pe, s, (name, 0))
                pe.wait_ge(s_norm, norms(s, kind))
                for t in range(TT):
                    last = nc.tensor.transpose(bank[:, t * P:(t + 1) * P], xh[:, t * D:(t + 1) * D], ident[:, :])
                last.then_inc(full, 1)

            def pe_up(pe, s, n, layer):
                bank, full = acquire(pe, s, ("up", n))
                emptied(pe, s, ("turn_ff", 0))
                for c in range(2):
                    f = (2 * n + c) * P
                    last = nc.tensor.matmul(bank[:, c * T:(c + 1) * T], w1[:, layer, f:f + P], xnT[:, MKV:J],
                                            start=True, stop=True)
                last.then_inc(full, 1)

            def pe_down(pe, s, layer):
                bank, full = acquire(pe, s, ("down", 0))
                emptied(pe, s, ("up", 1))
                for t in range(TT):
                    for c in range(FC):
                        nc.tensor.matmul(bank[:, t * D:(t + 1) * D], gT[:, c, t * P:(t + 1) * P], w2[:, layer, c, :],
                                         start=(c == 0), stop=False)
                    last = nc.tensor.matmul(bank[:, t * D:(t + 1) * D], ones[0:1, :], b2[0:1, layer, :],
                                            start=False, stop=True)
                last.then_inc(full, 1)

            def pe_qk(pe, s, c, layer):
                bank, full = acquire(pe, s, ("qk", c))
                emptied(pe, s, ("turn_qkv", 0))
                nc.tensor.matmul(bank[:, 0:T], wq[:, layer, c * P:(c + 1) * P], xnT[:, MKV:J], start=True, stop=True)
                nc.tensor.matmul(bank[:, T:2 * T], wk[:, layer, c * P:(c + 1) * P], xnT[:, MKV:J],
                                 start=True, stop=True).then_inc(full, 1)

            def pe_v(pe, s, n, layer):
                r, cols = n // 2, slice((n % 2) * 512, (n % 2 + 1) * 512)
                m = min(P, J - r * P)
                bank, full = acquire(pe, s, ("v", n))
                nc.tensor.matmul(bank[0:m, :], xnT[:, r * P:r * P + m], wv[:, layer, cols],
                                 start=True, stop=True).then_inc(full, 1)

            def pe_side(pe, s, name, n):
                if name == "dots1":
                    pe_dots(pe, s, 1, n)
                elif name == "dots0":
                    pe_dots(pe, s, 0, n)
                elif name == "av1":
                    pe_av(pe, s, 1, n, (s - 1) % 2)
                elif name == "av0":
                    pe_av(pe, s, 0, n, s % 2)
                elif name == "wo1":
                    pe_wo(pe, s, 1, done[s])
                elif name == "wo0":
                    pe_wo(pe, s, 0, now[s])
                elif name == "turn_ff":
                    pe_turn(pe, s, name, "ff")
                elif name == "turn_qkv":
                    pe_turn(pe, s, name, "qkv")
                elif name == "up":
                    pe_up(pe, s, n, done[s])
                elif name == "down":
                    pe_down(pe, s, done[s])
                elif name == "qk":
                    pe_qk(pe, s, n, coming[s])
                elif name == "v":
                    pe_v(pe, s, n, coming[s])

            def pe_mix(pe, n):
                w, bank = width(n % TILES), mix_bank[n % 2]
                pe.wait_ge(s_gath[n % DR], 16 * (n // DR + 1))
                wait(pe, s_x, n - 1)
                nc.tensor.matmul(bank[:, 0:w], pre[:, now[n // TILES], :], gathered[:, n % DR, 0:w],
                                 start=True, stop=True).then_inc(s_mix, 1)

            def pe_post(pe, n):
                pe.wait_ge(s_spost, n + 1)
                wait(pe, s_p, n - 1)
                for k, (j, m) in enumerate(key_chunks(width(n % TILES))):
                    last = nc.tensor.matmul(post_bank[n % 2][0:m, k * P:(k + 1) * P], e[:, n % ES, j:j + m],
                                            spost[:, n % 2, :], start=True, stop=True)
                last.then_inc(s_post, 1)

            def act_side(act, s, name, n):
                if name in ("wo0", "wo1", "down") or not takes_bank((name, n + 1)) and n % 2 == 0:
                    return
                if name in ("av0", "av1"):
                    bank, free = filled(act, s, (name, n - 1))
                    act.copy(oT[:, 2 * (n - 1):2 * (n - 1) + 4, :].rearrange("p c i -> p (c i)"), bank[:, :]) \
                       .then_inc(free, 1)
                    return
                bank, free = filled(act, s, (name, n))
                if name in ("dots0", "dots1"):
                    half = int(name[4])
                    act.copy(dots[half][:, n, :], bank[:, 0:WI[half]]).then_inc(free, 1)
                elif name in ("turn_ff", "turn_qkv"):
                    row, layer = (2, done[s]) if name == "turn_ff" else (0, coming[s])
                    act.activation(xnT[:, MKV:J], bank[:, 0:T], ACT.Identity, bias=gains[:, row + 1, layer:layer + 1],
                                   scale=gains[:, row, layer:layer + 1]).then_inc(free, 1)
                elif name == "up":
                    for c in range(2):
                        f = 2 * n + c
                        last = act.activation(gT[:, f, :], bank[:, c * T:(c + 1) * T], ACT.Gelu,
                                              bias=b1[:, done[s], f:f + 1])
                    last.then_inc(free, 1)
                elif name == "qk":
                    act.mul(qT[:, n, :], bank[:, 0:T], float(DH) ** -0.5)
                    act.copy(kT[:, n, MKV:J], bank[:, T:2 * T]).then_inc(free, 1)
                elif name == "v":
                    r, m = n // 2, min(P, J - n // 2 * P)
                    act.copy(v[0:m, (s + 1) % 2, r, (n % 2) * 512:(n % 2 + 1) * 512], bank[0:m, :]).then_inc(free, 1)

            def act_copy(act, n):
                w = width(n % TILES)
                act.wait_ge(s_mix, n + 1)
                wait(act, s_r, n + 1 - XS)
                act.copy(mixed[:, n % XS, 0:w], mix_bank[n % 2][:, 0:w]).then_inc(s_x, 1)

            def act_exp(act, n):
                w = width(n % TILES)
                act.wait_ge(s_nmax, n + 1)
                if w <= TOPK:
                    wait(act, s_r, n - 1)
                    act.activation(e[:, n % ES, 0:w], mixed[:, n % XS, 0:w], ACT.Exp, bias=nmax[:, n % XS:n % XS + 1],
                                   accum_out=total[:, n % 2:n % 2 + 1]).then_inc(s_e, 1)
                else:
                    act.activation(e[:, n % ES, 0:w], mixed[:, n % XS, 0:w], ACT.Exp,
                                   bias=nmax[:, n % XS:n % XS + 1]).then_inc(s_e, 1)

            def act_probs(act, n):
                t = n % TILES
                half, at = t // HALF, ROWS * (t % HALF)
                act.wait_ge(s_post, n + 1)
                for k, (j, m) in enumerate(key_chunks(width(t))):
                    last = act.copy(pT[half][k][0:m, :, at:at + ROWS],
                                    post_bank[n % 2][0:m, k * P:(k + 1) * P].rearrange("p (h i) -> p h i", i=ROWS))
                last.then_inc(s_p, 1)

            chain = [0]

            def link(ins):
                ins.then_inc(s_dve, 1)
                chain[0] += 1
                return chain[0]

            def dve_own(dve):
                dve.wait_ge(s_dve, chain[0])

            def dve_top(dve, tiles_at_once):
                w = {n: width(n % TILES) for n in tiles_at_once}
                at = {}
                for n in tiles_at_once:
                    dve.wait_ge(s_masked, n + 1)
                    wait(dve, s_nmax, n + 1 - XS)
                    dve.max(top[:, n % XS, 0:8], mixed[:, n % XS, 0:w[n]]).then_inc(s_max, 1)
                picky = [n for n in tiles_at_once if w[n] > TOPK]
                for r in range(8, TOPK, 8):
                    for n in picky:
                        if r == 8:
                            dve.wait_ge(s_max, n + 1)
                        else:
                            dve.wait_ge(s_dve, at[n])
                        source = mixed[:, n % XS, 0:w[n]] if r == 8 else left[:, n % 2, 0:w[n]]
                        at[n] = link(dve.match_replace(left[:, n % 2, 0:w[n]], top[:, n % XS, r - 8:r], source, TAKEN))
                    for n in picky:
                        dve.wait_ge(s_dve, at[n])
                        at[n] = link(dve.max(top[:, n % XS, r:r + 8], left[:, n % 2, 0:w[n]]))
                for n in picky:
                    dve.wait_ge(s_e, n + 1)
                    dve.wait_ge(s_dve, at[n])
                    at[n] = link(dve.scalar_tensor_tensor(
                        out=e[:, n % ES, 0:w[n]], in0=mixed[:, n % XS, 0:w[n]], scalar=top[:, n % XS, TOPK - 1:TOPK],
                        in1=e[:, n % ES, 0:w[n]], op0=ALU.is_ge, op1=ALU.mult, accum_out=total[:, n % 2:n % 2 + 1]))
                for n in tiles_at_once:
                    if n in picky:
                        dve.wait_ge(s_dve, at[n])
                    else:
                        dve.wait_ge(s_e, n + 1)
                    wait(dve, s_spost, n - 1)
                    dve.reciprocal(rtotal[:, n % 2:n % 2 + 1], total[:, n % 2:n % 2 + 1]).then_inc(s_r, 1)

            def dve_stats(dve, s, kind, source):
                k = norms(s, kind) - 1
                for t in range(TT):
                    link(dve.bn_stats(bst[:, t, :], source[:, t * D:(t + 1) * D]))
                dve_own(dve)
                for t in range(TT):
                    last = dve.bn_aggr(mv[:, k % 2, t, :], bst[:, t, :])
                last.then_inc(s_stats, 1)
                dve.wait_ge(s_stats, k + 1)

            def dve_wo(dve, s, half, stream):
                bank, free = filled(dve, s, (f"wo{half}", 0))
                part = z[:, stream, half * D:(half + 1) * D]
                dve.tensor_tensor(part, part, bank[:, 0:D], ALU.add).then_inc(free, 1)

            def dve_down(dve, s):
                stream = (s - 1) % 2
                bank, free = filled(dve, s, ("down", 0))
                dve.tensor_tensor(z[:, stream, :], z[:, stream, :], bank[:, 0:TT * D], ALU.add).then_inc(free, 1)
                if done[s] == DEPTH - 1:
                    emptied(dve, s, ("down", 0))
                    here = x[:, bass.ds(x_done(s), 1), :]
                    link(dve.tensor_tensor(here, here, z[:, stream:stream + 1, :], ALU.add))

            pooled = [0]

            def pool_link(pool, ins):
                ins.then_inc(s_pool, 1)
                pooled[0] += 1
                pool.wait_ge(s_pool, pooled[0])

            def pool_bring(pool, s):
                if (s, "turn_ff", 0) in turns.at:
                    filled(pool, s, ("turn_ff", 0))
                pool.tensor_copy(xh[:, None, :], x[:, bass.ds(x_new(s), 1), :]).then_inc(s_xin, 1)

            def pool_norm(pool, s, kind, source, to):
                k = norms(s, kind) - 1
                m = mv[:, k % 2, :, :]
                before = {"ff": (s - 1, "turn_qkv", 0), "qkv": (s, "turn_ff", 0)}.get(kind)
                if before in turns.at:
                    filled(pool, before[0], before[1:])
                pool.wait_ge(s_stats, k + 1)
                pool_link(pool, pool.tensor_scalar(vare[:, :], m[:, :, 1], 1.0, EPS, ALU.mult, ALU.add))
                pool_link(pool, pool.tensor_tensor(rstd[:, k % 2, :], vare[:, :], minus_half[:, :], ALU.pow))
                pool_link(pool, pool.tensor_tensor(shift[:, k % 2, :], m[:, :, 0], rstd[:, k % 2, :], ALU.mult))
                for t in range(TT):
                    last = pool.tensor_scalar(to[:, t * D:(t + 1) * D], source[:, t * D:(t + 1) * D],
                                              rstd[:, k % 2, t:t + 1], shift[:, k % 2, t:t + 1], ALU.mult, ALU.subtract)
                last.then_inc(s_norm, 1)
                pool.wait_ge(s_norm, k + 1)

            def pool_nmax(pool, n):
                pool.wait_ge(s_max, n + 1)
                wait(pool, s_e, n + 1 - XS)
                pool.tensor_scalar(nmax[:, n % XS:n % XS + 1], top[:, n % XS, 0:1], -1.0, 1.0, ALU.mult, ALU.mult) \
                    .then_inc(s_nmax, 1)

            def pool_mask(pool, n):
                w = width(n % TILES)
                pool.wait_ge(s_x, n + 1)
                edge = mixed[:, n % XS, w - ROWS:w]
                pool.tensor_tensor(edge, edge, causal[:, :], ALU.add).then_inc(s_masked, 1)

            def pool_spost(pool, n):
                pool.wait_ge(s_r, n + 1)
                wait(pool, s_post, n - 1)
                pool.tensor_scalar(spost[:, n % 2, :], post[:, now[n // TILES], :], rtotal[:, n % 2:n % 2 + 1], 1.0,
                                   ALU.mult, ALU.mult).then_inc(s_spost, 1)

            with nc.Block() as block:
                @block.sync
                def _(sp):
                    if not tiles and ("v", 1) in jobs_of_steps[0][1]:
                        sp_vmem(sp, jobs_of_steps[0][0])
                    for n in range(tiles):
                        s, t = n // TILES, n % TILES
                        if t == 0:
                            emptied(sp, s - 1, ("dots0", H - 1))
                        if t == HALF:
                            emptied(sp, s, ("dots1", H - 1))
                        wait(sp, s_mix, n + 1 - DR)
                        i = ROWS * (t % HALF)
                        if t == 4 and s > 0:
                            sp_vmem(sp, s - 1)
                        sp.dma_start(gathered[:, n % DR, 0:width(t)],
                                     dots[t // HALF][i:i + ROWS, :, 0:width(t)]).then_inc(s_gath[n % DR], 16)

                    if tiles:
                        sp_vmem(sp, STEPS - 1)
                    wait(sp, s_vmem, 16 * vmems(STEPS))

                @block.tensor
                def _(pe):
                    if not tiles:
                        for s, jobs in jobs_of_steps:
                            for name, k in jobs:
                                pe_side(pe, s, name, k)
                        return
                    for n in range(4):
                        pe_mix(pe, n)
                    for n in range(0, tiles, 2):
                        if n:
                            pe_post(pe, n - 2)
                            pe_post(pe, n - 1)
                        if n + 4 < tiles:
                            pe_mix(pe, n + 4)
                            pe_mix(pe, n + 5)
                        for name, k in PLAN[n % TILES] + PLAN[n % TILES + 1]:
                            pe_side(pe, n // TILES, name, k)
                    pe_post(pe, tiles - 2)
                    pe_post(pe, tiles - 1)

                @block.scalar
                def _(act):
                    if not tiles:
                        for s, jobs in jobs_of_steps:
                            for name, k in jobs:
                                act_side(act, s, name, k)
                        return
                    act_copy(act, 0)
                    act_copy(act, 1)
                    for n in range(0, tiles, 2):
                        if n + 2 < tiles:
                            act_copy(act, n + 2)
                            act_copy(act, n + 3)
                        act_exp(act, n)
                        act_exp(act, n + 1)
                        if n:
                            act_probs(act, n - 2)
                            act_probs(act, n - 1)
                        for name, k in PLAN[n % TILES] + PLAN[n % TILES + 1]:
                            act_side(act, n // TILES, name, k)
                    act_probs(act, tiles - 2)
                    act_probs(act, tiles - 1)

                def dve_finish(dve, s, at=None):
                    if at in (None, ADD_WO1):
                        dve_wo(dve, s, 1, (s - 1) % 2)
                        emptied(dve, s, ("wo1", 0))
                        dve_stats(dve, s, "ff", z[:, (s - 1) % 2, :])
                    if at in (None, ADD_DOWN):
                        dve_down(dve, s)

                def dve_prepare(dve, s, at=None):
                    if at in (None, ADD_DOWN) and (s, "new") in ln_order:
                        dve.wait_ge(s_xin, sum(1 for r, kind in ln_order if kind == "new" and r <= s))
                        dve_stats(dve, s, "new", xh)
                    if at in (None, STATS_QKV):
                        if (s, "new") in ln_order:
                            dve.wait_ge(s_norm, norms(s, "new"))
                        dve_stats(dve, s, "qkv", z[:, (s + 1) % 2, :])

                @block.vector
                def _(dve):
                    for s, jobs in jobs_of_steps:
                        if not tiles:
                            if ("wo1", 0) in jobs:
                                dve_finish(dve, s)
                            else:
                                dve_prepare(dve, s)
                            continue
                        for t in range(0, TILES, 2):
                            dve_finish(dve, s, t)
                            dve_prepare(dve, s, t)
                            if t == ADD_WO0:
                                dve_wo(dve, s, 0, s % 2)
                            dve_top(dve, (TILES * s + t, TILES * s + t + 1))

                def pool_finish(pool, s, at=None):
                    if at in (None, ADD_WO1):
                        pool_norm(pool, s, "ff", z[:, (s - 1) % 2, :], xh)

                def pool_prepare(pool, s, at=None):
                    if (s, "new") in ln_order:
                        if at in (None, BRING):
                            pool_bring(pool, s)
                        if at in (None, ADD_DOWN):
                            pool_norm(pool, s, "new", xh, z[:, (s + 1) % 2, :])
                    if at in (None, STATS_QKV):
                        pool_norm(pool, s, "qkv", z[:, (s + 1) % 2, :], xh)
                    if at in (None, KMEM):
                        pool_kmem(pool, s)

                @block.gpsimd
                def _(pool):
                    if tiles:
                        pool_mask(pool, 0)
                        pool_mask(pool, 1)
                    for s, jobs in jobs_of_steps:
                        if not tiles:
                            if ("wo1", 0) in jobs:
                                pool_finish(pool, s)
                            else:
                                pool_prepare(pool, s)
                            continue
                        for t in range(0, TILES, 2):
                            n = TILES * s + t
                            if n:
                                pool_spost(pool, n - 2)
                                pool_spost(pool, n - 1)
                            pool_nmax(pool, n)
                            pool_nmax(pool, n + 1)
                            if n + 2 < tiles:
                                pool_mask(pool, n + 2)
                                pool_mask(pool, n + 3)
                            pool_finish(pool, s, t)
                            pool_prepare(pool, s, t)
                    if tiles:
                        pool_spost(pool, tiles - 2)
                        pool_spost(pool, tiles - 1)

            for used in sems:
                nc.sync.sem_clear(used)
            nc.all_engine_barrier(sem_only=True)

        run([(-1, FIRST_JOBS)], [(-1, "new"), (-1, "qkv")], 0, None, lambda s: 1)
        step_jobs = [job for t in range(TILES) for job in PLAN[t]]
        order = [(0, "ff"), (0, "new"), (0, "qkv"), (1, "ff"), (1, "qkv"), (2, "ff"), (2, "qkv"),
                 (3, "ff"), (3, "new"), (3, "qkv")]
        with nc.Fori(0, B // 2) as pair:
            run([(s, step_jobs) for s in range(STEPS)], order, TILES * STEPS,
                lambda s: {0: pair * 2, 3: pair * 2 + 1}[s], lambda s: {0: pair * 2 + 2, 3: pair * 2 + 3}[s])
        run([(STEPS, LAST_JOBS)], [(STEPS, "ff")], 0, lambda s: B, None)


EXPERTS, HIDDEN = 8, 512
CAPACITY = int(T * 2.0 / EXPERTS) + 1
HC = HIDDEN // P
GROUP = 4
LH, LD = 16, D // 16
LV = LD + 1
ROWG = 4
LEPS = 1e-6


class Tail:

    def __init__(self, nc, ctx, x, ident, minus_half, mv, bst, rstd, vare):
        self.nc, self.x, self.ident, self.minus_half = nc, x, ident, minus_half
        self.mv, self.bst, self.rstd, self.vare = mv, bst, rstd, vare
        self.xh = ctx.enter_context(nc.sbuf_tensor("xh2", [P, 2, TT * D], F32))
        self.xnT = ctx.enter_context(nc.sbuf_tensor("xnT2", [P, 2, T], F32))
        names = ("s_agg", "s_stat", "s_vare", "s_rstd", "s_tok", "s_turned", "s_xnT")
        self.sems = [ctx.enter_context(nc.semaphore(name)) for name in names]
        self.agg, self.stat, self.var, self.rs, self.tok, self.turned, self.done = self.sems

    def dve_stats(self, dve, i, slot):
        wait(dve, self.stat, i)
        for t in range(TT):
            last = dve.bn_stats(self.bst[:, t, :], self.x[:, bass.ds(slot, 1), t * D:(t + 1) * D]
                                .rearrange("p o d -> p (o d)"))
        last.then_inc(self.agg, 1)
        dve.wait_ge(self.agg, i + 1)
        wait(dve, self.rs, i - 1)
        for t in range(TT):
            last = dve.bn_aggr(self.mv[:, i % 2, t, :], self.bst[:, t, :])
        last.then_inc(self.stat, 1)

    def pool_rstd(self, pool, i):
        pool.wait_ge(self.stat, i + 1)
        pool.tensor_scalar(self.vare[:, :], self.mv[:, i % 2, :, 1], 1.0, EPS, ALU.mult, ALU.add) \
            .then_inc(self.var, 1)
        pool.wait_ge(self.var, i + 1)
        wait(pool, self.tok, i - 1)
        pool.tensor_tensor(self.rstd[:, i % 2, :], self.vare[:, :], self.minus_half[:, :], ALU.pow) \
            .then_inc(self.rs, 1)
        pool.wait_ge(self.rs, i + 1)

    def dve_norm(self, dve, i, slot):
        dve.wait_ge(self.rs, i + 1)
        dve.wait_ge(self.stat, i + 1)
        wait(dve, self.turned, i - 1)
        for t in range(TT):
            last = dve.tensor_scalar(self.xh[:, i % 2, t * D:(t + 1) * D],
                                     self.x[:, bass.ds(slot, 1), t * D:(t + 1) * D].rearrange("p o d -> p (o d)"),
                                     self.mv[:, i % 2, t, 0:1], self.rstd[:, i % 2, t:t + 1],
                                     ALU.subtract, ALU.mult)
        last.then_inc(self.tok, 1)

    def pe_turn(self, pe, i, bank):
        pe.wait_ge(self.tok, i + 1)
        wait(pe, self.done, i - 1)
        for t in range(TT):
            last = pe.transpose(bank[:, t * P:(t + 1) * P], self.xh[:, i % 2, t * D:(t + 1) * D], self.ident[:, :])
        last.then_inc(self.turned, 1)

    def act_turn(self, act, i, bank, readers):
        act.wait_ge(self.turned, i + 1)
        for s, per in readers:
            wait(act, s, per * (i - 1))
        act.copy(self.xnT[:, i % 2, :], bank[:, 0:T]).then_inc(self.done, 1)


def clear(nc, sems):
    for used in sems:
        nc.sync.sem_clear(used)
    nc.all_engine_barrier(sem_only=True)


class Experts:

    def __init__(self, nc, a, ctx):
        def sb(name, shape):
            return ctx.enter_context(nc.sbuf_tensor(name, shape, F32))

        self.router = sb("router", [P, EXPERTS])
        self.w1 = sb("ew1", [P, EXPERTS, HIDDEN])
        self.w2 = sb("ew2", [P, EXPERTS, HC, D])
        self.b1 = sb("eb1", [P, EXPERTS, HC])
        self.b2 = sb("eb2", [EXPERTS, D])
        self.loads = [(self.router[:, :], a["router"]), (self.b1[:, :, :], a["eb1"]), (self.b2[:, :], a["eb2"])]
        for n in range(EXPERTS):
            self.loads.append((self.w1[:, n, :], a["ew1"][n]))
            self.loads.append((self.w2[:, n, :, :], a["ew2"][n].rearrange("(c p) n -> p c n", p=P)))
        self.xall = sb("xall", [P, B, T])
        self.score = sb("score", [P, TT, B, EXPERTS])
        self.one = sb("one_each", [P, TT, B])
        self.inv = sb("inv_each", [P, TT, B])
        self.turned = sb("sturn", [P, T])
        self.left = sb("sleft", [P, T])
        self.top = sb("stop", [P, -(-CAPACITY // 8) * 8])
        self.above = sb("above", [P, T])
        self.equal = sb("equal", [P, T])
        self.run_of = sb("run_of", [P, T])
        self.unit = sb("unit", [P, T])
        self.count = sb("count", [P, 1])
        self.room = sb("room", [P, 1])
        self.gate = sb("gate", [P, TT, B, EXPERTS])
        self.g = sb("g", [P, 2, TT, EXPERTS])
        self.gT = sb("gT8", [EXPERTS, 2, T])
        self.xs = sb("xs", [P, 2, T])
        self.hT = sb("hT", [P, 2, HC, T])
        self.acc = sb("eacc", [P, 2, TT * D])
        names = ("s_logit", "s_score", "s_xall", "s_link", "s_exp", "s_pe", "s_act", "s_g", "s_gt", "s_gT", "s_bias",
                 "s_init", "s_xs", "s_up", "s_h", "s_down", "s_acc", "s_unit")
        self.sem = {name: ctx.enter_context(nc.semaphore("e" + name)) for name in names}

    def route(self, nc, f, banks):
        s = self.sem
        turn_bank, logit_bank = banks[0:2], banks[2:4]
        with nc.Fori(0, B // GROUP) as group:
            with nc.Block() as block:
                def pool_keep(pool, i):
                    pool.wait_ge(f.done, i + 1)
                    pool.tensor_copy(self.xall[:, bass.ds(group * GROUP + i, 1), :], f.xnT[:, i % 2, None, :]) \
                        .then_inc(s["s_xall"], 1)

                @block.vector
                def _(dve):
                    f.dve_stats(dve, 0, group * GROUP + 1)
                    for i in range(GROUP):
                        if i + 1 < GROUP:
                            f.dve_stats(dve, i + 1, group * GROUP + i + 2)
                        f.dve_norm(dve, i, group * GROUP + i + 1)

                @block.gpsimd
                def _(pool):
                    for i in range(GROUP):
                        f.pool_rstd(pool, i)
                        if i:
                            pool_keep(pool, i - 1)
                    pool_keep(pool, GROUP - 1)

                @block.tensor
                def _(pe):
                    f.pe_turn(pe, 0, turn_bank[0])
                    for i in range(GROUP):
                        if i + 1 < GROUP:
                            f.pe_turn(pe, i + 1, turn_bank[(i + 1) % 2])
                        pe.wait_ge(f.done, i + 1)
                        wait(pe, s["s_score"], i - 1)
                        for t in range(TT):
                            last = pe.matmul(logit_bank[i % 2][:, t * EXPERTS:(t + 1) * EXPERTS],
                                             f.xnT[:, i % 2, t * P:(t + 1) * P], self.router[:, :],
                                             start=True, stop=True)
                        last.then_inc(s["s_logit"], 1)

                @block.scalar
                def _(act):
                    for i in range(GROUP):
                        f.act_turn(act, i, turn_bank[i % 2], [(s["s_logit"], 1), (s["s_xall"], 1)])
                        act.wait_ge(s["s_logit"], i + 1)
                        act.copy(self.score[:, :, bass.ds(group * GROUP + i, 1), :],
                                 logit_bank[i % 2][:, 0:TT * EXPERTS]
                                 .rearrange("p (t o e) -> p t o e", t=TT, o=1)).then_inc(s["s_score"], 1)
            clear(nc, f.sems + list(s.values()))

    def choose(self, nc, f, banks):
        s = self.sem
        flat = [P, TT * B, EXPERTS]
        score = self.score[:, :, :, :].rearrange("p t b e -> p (t b) e")
        one = self.one[:, :, :].rearrange("p t b -> p (t b)")
        inv = self.inv[:, :, :].rearrange("p t b -> p (t b)")
        with nc.Block() as block:
            @block.vector
            def _(dve):
                count = [0]

                def link(ins):
                    ins.then_inc(s["s_link"], 1)
                    count[0] += 1
                    dve.wait_ge(s["s_link"], count[0])

                link(dve.memset(self.unit[:, :], 1.0))
                link(dve.tensor_reduce(one, score, mybir.AxisListType.X, ALU.max))
                dve.tensor_tensor(score, score, one[:, :, None].broadcast_to(flat), ALU.subtract) \
                   .then_inc(s["s_unit"], 1)
                dve.wait_ge(s["s_exp"], 1)
                link(dve.tensor_reduce(one, score, mybir.AxisListType.X, ALU.add))
                link(dve.reciprocal(inv, one))
                dve.tensor_tensor(score, score, inv[:, :, None].broadcast_to(flat), ALU.mult) \
                   .then_inc(s["s_unit"], 1)
                dve.wait_ge(s["s_act"], 1)
                source = self.turned[:, :]
                for r in range(0, CAPACITY, 8):
                    link(dve.max(self.top[:, r:r + 8], source))
                    if r + 8 < CAPACITY:
                        link(dve.match_replace(self.left[:, :], self.top[:, r:r + 8], source, TAKEN))
                        source = self.left[:, :]
                last = self.top[:, CAPACITY - 1:CAPACITY]
                link(dve.tensor_scalar(self.above[:, :], self.turned[:, :], last, None, ALU.is_gt, ALU.add,
                                       accum_out=self.count[:, :]))
                link(dve.tensor_scalar(self.equal[:, :], self.turned[:, :], last, None, ALU.is_equal))
                link(dve.tensor_scalar(self.room[:, :], self.count[:, :], -1.0, float(CAPACITY), ALU.mult, ALU.add))
                link(dve.tensor_tensor_scan(self.run_of[:, :], self.unit[:, :], self.equal[:, :], 0.0,
                                            ALU.mult, ALU.add))
                link(dve.scalar_tensor_tensor(out=self.equal[:, :], in0=self.run_of[:, :], scalar=self.room[:, :],
                                              in1=self.equal[:, :], op0=ALU.is_le, op1=ALU.mult))
                link(dve.tensor_tensor(self.above[:, :], self.above[:, :], self.equal[:, :], ALU.add))
                dve.tensor_tensor(self.turned[:, :], self.turned[:, :], self.above[:, :], ALU.mult) \
                   .then_inc(s["s_unit"], 1)

            @block.scalar
            def _(act):
                act.wait_ge(s["s_unit"], 1)
                act.activation(score, score, ACT.Exp).then_inc(s["s_exp"], 1)
                act.wait_ge(s["s_pe"], 1)
                act.copy(self.turned[:, :], banks[0][:, 0:T]).then_inc(s["s_act"], 1)
                act.wait_ge(s["s_pe"], 2)
                act.copy(self.gate[:, :, :, :].rearrange("p t b e -> p (t b e)"), banks[1][:, 0:T]) \
                   .then_inc(s["s_act"], 1)

            @block.tensor
            def _(pe):
                pe.wait_ge(s["s_unit"], 2)
                for t in range(TT):
                    last = pe.transpose(banks[0][:, t * P:(t + 1) * P],
                                        self.score[:, t, :, :].rearrange("p b e -> p (b e)"), f.ident[:, :])
                last.then_inc(s["s_pe"], 1)
                pe.wait_ge(s["s_unit"], 3)
                for t in range(TT):
                    last = pe.transpose(banks[1][:, t * P:(t + 1) * P], self.turned[:, t * P:(t + 1) * P],
                                        f.ident[:, :])
                last.then_inc(s["s_pe"], 1)
        clear(nc, list(s.values()))

    def mix(self, nc, f, banks):
        s = self.sem
        up_bank, down_bank, turn_bank, bias_bank = banks[0:4], banks[4:6], banks[6], banks[7]
        last_k = GROUP * EXPERTS - 1

        with nc.Fori(0, B // GROUP) as group:
            def prepare(eng, stage, i):
                if stage == "gates":
                    eng.tensor_copy(self.g[:, i % 2, :, :].rearrange("p t (o e) -> p t o e", o=1),
                                    self.gate[:, :, bass.ds(group * GROUP + i, 1), :]).then_inc(s["s_g"], 1)
                elif stage == "turn":
                    eng.wait_ge(s["s_g"], i + 1)
                    wait(eng, s["s_gT"], i)
                    for t in range(TT):
                        last = eng.transpose(turn_bank[0:EXPERTS, t * P:(t + 1) * P], self.g[:, i % 2, t, :],
                                             f.ident[:, :])
                    last.then_inc(s["s_gt"], 1)
                elif stage == "copy":
                    eng.wait_ge(s["s_gt"], i + 1)
                    eng.copy(self.gT[:, i % 2, :], turn_bank[0:EXPERTS, 0:T]).then_inc(s["s_gT"], 1)
                elif stage == "bias":
                    eng.wait_ge(s["s_gT"], i + 1)
                    wait(eng, s["s_init"], i)
                    for t in range(TT):
                        last = eng.matmul(bias_bank[:, t * D:(t + 1) * D], self.gT[:, i % 2, t * P:(t + 1) * P],
                                          self.b2[:, :], start=True, stop=True)
                    last.then_inc(s["s_bias"], 1)
                elif stage == "start":
                    eng.wait_ge(s["s_bias"], i + 1)
                    eng.tensor_tensor(self.acc[:, i % 2, None, :], bias_bank[:, None, 0:TT * D],
                                      f.x[:, bass.ds(group * GROUP + i + 1, 1), :], ALU.add).then_inc(s["s_init"], 1)

            def pe_up(pe, k):
                i, n = k // EXPERTS, k % EXPERTS
                if n == 0:
                    pe.wait_ge(s["s_xs"], i + 1)
                for half in range(2):
                    wait(pe, s["s_h"], 2 * k + half - 3)
                    for c in range(2):
                        h = (2 * half + c) * P
                        last = pe.matmul(up_bank[(2 * k + half) % 4][:, c * T:(c + 1) * T],
                                         self.w1[:, n, h:h + P], self.xs[:, i % 2, :], start=True, stop=True)
                    last.then_inc(s["s_up"], 1)

            with nc.Block() as block:
                @block.gpsimd
                def _(pool):
                    for i in range(GROUP):
                        wait(pool, s["s_up"], 2 * EXPERTS * (i - 1))
                        pool.tensor_copy(self.xs[:, i % 2, None, :], self.xall[:, bass.ds(group * GROUP + i, 1), :]) \
                            .then_inc(s["s_xs"], 1)

                @block.tensor
                def _(pe):
                    prepare(pe, "turn", 0)
                    pe_up(pe, 0)
                    prepare(pe, "bias", 0)
                    for k in range(last_k + 1):
                        i, n = k // EXPERTS, k % EXPERTS
                        if k < last_k:
                            pe_up(pe, k + 1)
                        pe.wait_ge(s["s_h"], 2 * k + 2)
                        wait(pe, s["s_acc"], k - 1)
                        for t in range(TT):
                            for c in range(HC):
                                last = pe.matmul(down_bank[k % 2][:, t * D:(t + 1) * D],
                                                 self.hT[:, k % 2, c, t * P:(t + 1) * P], self.w2[:, n, c, :],
                                                 start=(c == 0), stop=(c == HC - 1))
                        last.then_inc(s["s_down"], 1)
                        if i + 1 < GROUP and n == 3:
                            prepare(pe, "turn", i + 1)
                        if i + 1 < GROUP and n == 5:
                            prepare(pe, "bias", i + 1)

                @block.scalar
                def _(act):
                    prepare(act, "copy", 0)
                    for k in range(last_k + 1):
                        i, n = k // EXPERTS, k % EXPERTS
                        wait(act, s["s_down"], k - 1)
                        for half in range(2):
                            act.wait_ge(s["s_up"], 2 * k + half + 1)
                            for c in range(2):
                                h = 2 * half + c
                                last = act.activation(self.hT[:, k % 2, h, :],
                                                      up_bank[(2 * k + half) % 4][:, c * T:(c + 1) * T],
                                                      ACT.Gelu, bias=self.b1[:, n, h:h + 1])
                            last.then_inc(s["s_h"], 1)
                        if i + 1 < GROUP and n == 4:
                            prepare(act, "copy", i + 1)

                @block.vector
                def _(dve):
                    prepare(dve, "gates", 0)
                    prepare(dve, "start", 0)
                    for k in range(last_k + 1):
                        i, n = k // EXPERTS, k % EXPERTS
                        if i + 1 < GROUP and n == 2:
                            prepare(dve, "gates", i + 1)
                        dve.wait_ge(s["s_down"], k + 1)
                        dve.wait_ge(s["s_init"], i + 1)
                        wait(dve, s["s_acc"], k)
                        for t in range(TT):
                            part = self.acc[:, i % 2, t * D:(t + 1) * D]
                            to = part if n < EXPERTS - 1 else \
                                f.x[:, bass.ds(group * GROUP + i + 1, 1), t * D:(t + 1) * D] \
                                .rearrange("p o d -> p (o d)")
                            last = dve.scalar_tensor_tensor(out=to, in0=down_bank[k % 2][:, t * D:(t + 1) * D],
                                                            scalar=self.g[:, i % 2, t, n:n + 1], in1=part,
                                                            op0=ALU.mult, op1=ALU.add)
                        last.then_inc(s["s_acc"], 1)
                        if i + 1 < GROUP and n == 6:
                            prepare(dve, "start", i + 1)
            clear(nc, list(s.values()))

    def run(self, nc, f, banks):
        self.route(nc, f, banks)
        self.choose(nc, f, banks)
        self.mix(nc, f, banks)


class Linear:

    def __init__(self, nc, a, ctx):
        def sb(name, shape):
            return ctx.enter_context(nc.sbuf_tensor(name, shape, F32))

        self.wT = sb("lwT", [P, 5, D])
        self.nbg = sb("nbg", [P, 1])
        self.loads = [(self.wT[:, n, :], a[name]) for n, name in enumerate(("lq", "lk", "lg", "lv", "lo"))]
        self.loads.append((self.nbg[:, :], a["lbg"]))
        self.head = sb("lhead", [P, LH])
        self.fourth = sb("lfourth", [P, ROWG])
        self.tri = sb("ltri", [P, P])
        self.mag = sb("lmag", [P, 2, 2 * T])
        self.soft = sb("lsoft", [P, 2, 2 * T])
        self.sig = sb("lsig", [P, 2, T])
        self.qf = sb("lqf", [P, 2, T])
        self.qx = sb("lqx", [P, 2, ROWG, T])
        self.vx = sb("lvx", [P, 2, TT, LH, LV])
        self.kf = sb("lkf", [P, 2, P])
        self.state = sb("lstate", [P, 2, LH, LV])
        self.s = sb("ls", [P, TT, LH // ROWG, ROWG, P])
        self.den = sb("lden", [P, 2, TT, LH])
        self.o = sb("lo_", [P, 2, TT * D])
        self.oT = sb("loT", [P, 2, T])
        names = ("s_proj", "s_mag", "s_ln", "s_soft", "s_eg", "s_v", "s_qf", "s_qx", "s_kt", "s_kf", "s_st", "s_state",
                 "s_sc", "s_s", "s_o", "s_den", "s_out", "s_ot", "s_oT", "s_y", "s_x", "s_link")
        self.sem = {name: ctx.enter_context(nc.semaphore("l" + name)) for name in names}

    def run(self, nc, f, banks):
        s = self.sem
        qk_bank, gv_bank, misc, o_bank, s_bank = banks[0], banks[1], banks[2], banks[3], banks[4:8]
        with nc.Fori(0, B // GROUP) as group:
            with nc.Block() as block:
                def slot(i):
                    return group * GROUP + i + 1

                @block.gpsimd
                def _(pool):
                    for i in range(GROUP):
                        f.pool_rstd(pool, i)

                def pe_project(pe, i):
                    wait(pe, s["s_v"], i)
                    f.pe_turn(pe, i, gv_bank)
                    pe.wait_ge(f.done, i + 1)
                    wait(pe, s["s_soft"], i)
                    for n in range(2):
                        last = pe.matmul(qk_bank[:, n * T:(n + 1) * T], self.wT[:, n, :], f.xnT[:, i % 2, :],
                                         start=True, stop=True)
                    last.then_inc(s["s_proj"], 1)
                    pe.matmul(gv_bank[:, 0:T], self.wT[:, 2, :], f.xnT[:, i % 2, :], start=True, stop=True)
                    for t in range(TT):
                        last = pe.matmul(gv_bank[:, T + t * D:T + (t + 1) * D], f.xnT[:, i % 2, t * P:(t + 1) * P],
                                         self.wT[:, 3, :], start=True, stop=True)
                    last.then_inc(s["s_proj"], 1)

                def pe_scores(pe, i):
                    pe.wait_ge(s["s_soft"], i + 1)
                    wait(pe, s["s_oT"], i)
                    pe.transpose(misc[:, 0:P], self.soft[:, i % 2, T:T + P], f.ident[:, :]) \
                      .then_inc(s["s_kt"], 1)
                    pe.wait_ge(s["s_qx"], i + 1)
                    for t in range(TT):
                        for r in range(LH // ROWG):
                            wait(pe, s["s_s"], (2 * i + t - 1) * (LH // ROWG) + r + 1)
                            lo = r * ROWG * LD
                            pe.matmul(s_bank[r][:, :], self.soft[lo:lo + ROWG * LD, i % 2, T + t * P:T + (t + 1) * P],
                                      self.qx[lo:lo + ROWG * LD, i % 2, :, t * P:(t + 1) * P],
                                      start=True, stop=True).then_inc(s["s_sc"], 1)
                    pe.wait_ge(s["s_kf"], i + 1)
                    pe.wait_ge(s["s_v"], i + 1)
                    wait(pe, s["s_out"], i)
                    wait(pe, s["s_state"], i)
                    pe.matmul(o_bank[:, TT * LH * LV:(TT + 1) * LH * LV], self.kf[:, i % 2, :],
                              self.vx[:, i % 2, 0, :, :].rearrange("p h v -> p (h v)"), start=True, stop=True) \
                      .then_inc(s["s_st"], 1)

                def pe_values(pe, i):
                    pe.wait_ge(s["s_state"], i + 1)
                    for t in range(TT):
                        pe.wait_ge(s["s_s"], (2 * i + t + 1) * (LH // ROWG))
                        if t:
                            pe.matmul(o_bank[:, t * LH * LV:(t + 1) * LH * LV], self.qf[:, i % 2, t * P:(t + 1) * P],
                                      self.state[:, i % 2, :, :].rearrange("p h v -> p (h v)"), start=True, stop=True)
                        for h in range(LH):
                            at = (t * LH + h) * LV
                            last = pe.matmul(o_bank[:, at:at + LV], self.s[:, t, h // ROWG, h % ROWG, :],
                                             self.vx[:, i % 2, t, h, :], start=(t == 0), stop=True,
                                             skip_group_check=(t > 0))
                    last.then_inc(s["s_o"], 1)

                def pe_out(pe, i):
                    pe.wait_ge(s["s_out"], i + 1)
                    pe.wait_ge(s["s_kf"], i + 1)
                    for t in range(TT):
                        last = pe.transpose(misc[:, t * P:(t + 1) * P], self.o[:, i % 2, t * D:(t + 1) * D],
                                            f.ident[:, :])
                    last.then_inc(s["s_ot"], 1)
                    pe.wait_ge(s["s_oT"], i + 1)
                    for t in range(TT):
                        last = pe.matmul(o_bank[:, t * D:(t + 1) * D], self.oT[:, i % 2, t * P:(t + 1) * P],
                                         self.wT[:, 4, :], start=True, stop=True)
                    last.then_inc(s["s_y"], 1)

                @block.tensor
                def _(pe):
                    pe_project(pe, 0)
                    for i in range(GROUP):
                        pe_scores(pe, i)
                        if i + 1 < GROUP:
                            pe_project(pe, i + 1)
                        pe_values(pe, i)
                        pe_out(pe, i)
                        pe.wait_ge(s["s_x"], i + 1)

                def act_project(act, i):
                    f.act_turn(act, i, gv_bank, [(s["s_proj"], 2)])
                    act.wait_ge(s["s_proj"], 2 * i + 1)
                    wait(act, s["s_soft"], i - 1)
                    act.activation(self.mag[:, i % 2, :], qk_bank[:, :], ACT.Abs).then_inc(s["s_mag"], 1)
                    act.wait_ge(s["s_mag"], 3 * i + 1)
                    act.activation(self.mag[:, i % 2, :], self.mag[:, i % 2, :], ACT.Exp, scale=-1.0) \
                       .then_inc(s["s_mag"], 1)
                    act.wait_ge(s["s_proj"], 2 * i + 2)
                    act.activation(self.sig[:, i % 2, :], gv_bank[:, 0:T], ACT.Exp, bias=self.nbg[:, :], scale=-1.0) \
                       .then_inc(s["s_eg"], 1)
                    act.wait_ge(s["s_mag"], 3 * i + 2)
                    act.activation(self.mag[:, i % 2, :], self.mag[:, i % 2, :], ACT.Ln, bias=1.0) \
                       .then_inc(s["s_mag"], 1)
                    act.copy(self.vx[:, i % 2, :, :, 0:LD].rearrange("p t h v -> p (t h) v"),
                             gv_bank[:, T:2 * T].rearrange("p (h v) -> p h v", v=LD)).then_inc(s["s_v"], 1)

                @block.scalar
                def _(act):
                    act_project(act, 0)
                    for i in range(GROUP):
                        act.wait_ge(s["s_kt"], i + 1)
                        act.copy(self.kf[:, i % 2, :], misc[:, 0:P]).then_inc(s["s_kf"], 1)
                        if i + 1 < GROUP:
                            act_project(act, i + 1)
                        act.wait_ge(s["s_ot"], i + 1)
                        act.copy(self.oT[:, i % 2, :], misc[:, 0:T]).then_inc(s["s_oT"], 1)

                linked = [0]

                def own(dve, ins):
                    ins.then_inc(s["s_link"], 1)
                    linked[0] += 1
                    dve.wait_ge(s["s_link"], linked[0])

                def dve_features(dve, i):
                    both = self.soft[:, i % 2, :]
                    dve.wait_ge(s["s_mag"], 3 * i + 3)
                    dve.scalar_tensor_tensor(out=both, in0=qk_bank[:, :], scalar=0.0, in1=self.mag[:, i % 2, :],
                                             op0=ALU.max, op1=ALU.add).then_inc(s["s_soft"], 1)
                    dve.wait_ge(s["s_eg"], i + 1)
                    sig = self.sig[:, i % 2, :]
                    own(dve, dve.tensor_scalar(sig, sig, 1.0, None, ALU.add))
                    own(dve, dve.reciprocal(sig, sig))
                    dve.wait_ge(s["s_soft"], i + 1)
                    dve.scalar_tensor_tensor(out=self.qf[:, i % 2, :], in0=sig, scalar=LEPS,
                                             in1=self.soft[:, i % 2, 0:T], op0=ALU.add, op1=ALU.mult) \
                       .then_inc(s["s_qf"], 1)
                    dve.wait_ge(s["s_qf"], i + 1)
                    for m in range(ROWG):
                        last = dve.tensor_scalar(self.qx[:, i % 2, m, :], self.qf[:, i % 2, :],
                                                 self.fourth[:, m:m + 1], None, ALU.mult)
                    last.then_inc(s["s_qx"], 1)

                def dve_scores(dve, i):
                    for t in range(TT):
                        if t == 0:
                            wait(dve, s["s_o"], i)
                        for r in range(LH // ROWG):
                            dve.wait_ge(s["s_sc"], (2 * i + t) * (LH // ROWG) + r + 1)
                            dve.tensor_tensor(self.s[:, t, r, :, :],
                                              s_bank[r][:, :].rearrange("p (m t) -> p m t", m=ROWG),
                                              self.tri[:, None, :].broadcast_to([P, ROWG, P]), ALU.mult) \
                               .then_inc(s["s_s"], 1)
                    dve.wait_ge(s["s_st"], i + 1)
                    dve.tensor_tensor(self.state[:, i % 2, :, :],
                                      o_bank[:, TT * LH * LV:(TT + 1) * LH * LV].rearrange("p (h v) -> p h v", v=LV),
                                      self.head[:, :, None].broadcast_to([P, LH, LV]), ALU.mult) \
                       .then_inc(s["s_state"], 1)

                def dve_out(dve, i):
                    dve.wait_ge(s["s_o"], i + 1)
                    wait(dve, s["s_ot"], i - 1)
                    o = o_bank[:, 0:TT * LH * LV].rearrange("p (h v) -> p h v", v=LV)
                    den = self.den[:, i % 2, :, :].rearrange("p t h -> p (t h)")
                    own(dve, dve.tensor_scalar(den, o[:, :, LD], LEPS, None, ALU.add))
                    own(dve, dve.reciprocal(den, den))
                    dve.tensor_tensor(self.o[:, i % 2, :].rearrange("p (h v) -> p h v", v=LD), o[:, :, 0:LD],
                                      den[:, :, None].broadcast_to([P, TT * LH, LD]), ALU.mult) \
                       .then_inc(s["s_out"], 1)
                    dve.wait_ge(s["s_y"], i + 1)
                    here = f.x[:, bass.ds(slot(i), 1), :]
                    dve.tensor_tensor(here, here, o_bank[:, None, 0:TT * D], ALU.add).then_inc(s["s_x"], 1)

                @block.vector
                def _(dve):
                    f.dve_stats(dve, 0, slot(0))
                    f.dve_norm(dve, 0, slot(0))
                    dve_features(dve, 0)
                    for i in range(GROUP):
                        if i + 1 < GROUP:
                            f.dve_stats(dve, i + 1, slot(i + 1))
                            f.dve_norm(dve, i + 1, slot(i + 1))
                        dve_scores(dve, i)
                        if i + 1 < GROUP:
                            dve_features(dve, i + 1)
                        dve_out(dve, i)
            clear(nc, f.sems + list(s.values()))


def tail(nc, a, x, ident, minus_half, mv, bst, rstd, vare, banks, s_tail, s_mask):
    with ExitStack() as ctx:
        f = Tail(nc, ctx, x, ident, minus_half, mv, bst, rstd, vare)
        experts = Experts(nc, a, ctx)
        linear = Linear(nc, a, ctx)
        loads = experts.loads + linear.loads
        with nc.Block() as block:
            @block.sync
            def _(sp):
                for to, source in loads:
                    sp.dma_start(to, source).then_inc(s_tail, 16)
                sp.wait_ge(s_tail, 16 * len(loads))

            @block.gpsimd
            def _(pool):
                pool.memset(linear.head[:, :], 1.0).then_inc(s_mask, 1)
                pool.memset(linear.tri[:, :], 1.0).then_inc(s_mask, 1)
                pool.memset(linear.vx[:, :, :, :, :], 1.0).then_inc(s_mask, 1)
                pool.wait_ge(s_mask, 2)
                pool.affine_select(out=linear.tri[:, :], in_=linear.tri[:, :], compare_op=ALU.is_ge, fill=0.0, base=0,
                                   pattern=[[1, P]], channel_multiplier=-1).then_inc(s_mask, 1)
                pool.affine_select(out=linear.head[:, :], in_=linear.head[:, :], compare_op=ALU.is_ge, fill=0.0,
                                   base=0, pattern=[[-LD, LH]], channel_multiplier=1).then_inc(s_mask, 1)
                pool.wait_ge(s_mask, 5)
                pool.affine_select(out=linear.head[:, :], in_=linear.head[:, :], compare_op=ALU.is_ge, fill=0.0,
                                   base=LD - 1, pattern=[[LD, LH]], channel_multiplier=-1).then_inc(s_mask, 1)

            @block.vector
            def _(dve):
                dve.wait_ge(s_mask, 6)
                dve.tensor_reduce(linear.fourth[:, :],
                                  linear.head[:, :].rearrange("p (r m) -> p m r", m=ROWG), mybir.AxisListType.X,
                                  ALU.add)
                dve.wait_ge(s_tail, 16 * len(loads))
                dve.tensor_scalar(linear.nbg[:, :], linear.nbg[:, :], -1.0, None, ALU.mult)

        experts.run(nc, f, banks)
        linear.run(nc, f, banks)
        experts.run(nc, f, banks)


def kernel(**inputs):
    import numpy as _np
    import concourse.bacc as _bacc
    from concourse import mybir as _mybir
    from concourse.bass_utils import run_bass_kernel_spmd as _run

    given = {name[len("L0_"):]: _np.ascontiguousarray(value) for name, value in inputs.items()}
    names = {"x": "attn_a_x", "wq": "attn_a_wq", "wk": "attn_a_wk",
             "wv": "attn_a_wv", "mem_v": "attn_a_mem_v", "pre": "attn_a_pre_proj", "post": "attn_a_post_proj",
             "wo": "attn_a_wo", "bo": "attn_a_bo", 
             "w1": "attn_a_w1", "w2": "attn_a_w2", "b2": "attn_a_b2",
             "ew1": "ffn_w1", "ew2": "ffn_w2", "eb2": "ffn_b2"}
    laid = {short: given[name] for short, name in names.items()}
    laid["gains"] = _np.ascontiguousarray(_np.stack(
        [given["attn_a_" + name] for name in ("ln1_g", "ln1_b", "ln2_g", "ln2_b")]).transpose(2, 0, 1))
    laid["b1"] = _np.ascontiguousarray(given["attn_a_b1"].reshape(DEPTH, FC, P).transpose(2, 0, 1))
    laid["router"] = _np.ascontiguousarray(given["ffn_router_w"].T)
    laid["eb1"] = _np.ascontiguousarray(given["ffn_b1"].reshape(EXPERTS, HC, P).transpose(2, 0, 1))
    for n in "qkgvo":
        laid["l" + n] = _np.ascontiguousarray(given["attn_b_W" + n].T)
    laid["lbg"] = given["attn_b_bg"].reshape(P, 1)
    laid["mem_kT"] = _np.ascontiguousarray(given["attn_a_mem_k"].transpose(0, 1, 3, 2))

    nc = _bacc.Bacc("TRN2", target_bir_lowering=False, num_devices=1)
    arrays, args = {}, {}
    for name, value in laid.items():
        arrays[f"in_{name}"] = value
        args[name] = nc.dram_tensor(f"in_{name}", value.shape, _mybir.dt.from_np(value.dtype), kind="ExternalInput").ap()
    out = nc.dram_tensor("out", (B, T, D), _mybir.dt.float32, kind="ExternalOutput").ap()
    program(nc, args, out)
    return _run(nc, [arrays], core_ids=[0]).results[0]["out"]
```

```python
from contextlib import ExitStack

import concourse.bass as bass
from concourse import mybir

ALU = mybir.AluOpType
ACT = mybir.ActivationFunctionType
F32 = mybir.dt.float32

P = 128
B, T, D = 16, 256, 128
TT = T // P
H, DH, MKV, TOPK = 16, 64, 32, 64
DEPTH = 2
NC_H = H * DH // P
J = MKV + T
FC = 4 * D // P
ROWS = P // H
TILES = T // ROWS
HALF = TILES // TT
PAIR = 4
STEPS = 2 * PAIR
WI = [MKV + P, J]
EPS = 1e-5
MASKED = -(2.0 ** 126)
TAKEN = -3.0e38
DR, XS, ES = 4, 6, 4


def width(t):
    return ROWS * (t + 1) + MKV


def key_chunks(w):
    return [(j, min(P, w - j)) for j in range(0, w, P)]


class Turns:

    def __init__(self, names, banks):
        self.at = {name: n for n, name in enumerate(names)}
        self.banks = banks

    def bank(self, name):
        return self.at[name] % self.banks

    def full(self, name):
        return self.at[name] // self.banks + 1

    def free(self, name):
        return self.at[name] // self.banks


def wait(eng, sem, value):
    if value > 0:
        eng.wait_ge(sem, value)


def side_plan(av_delay):
    plan = {t: [] for t in range(TILES)}
    for n in range(4):
        plan[2 + n // 2 * 2 + av_delay].append(("av1", n))
    for h in range(H):
        plan[6 + h // 4].append(("dots1", h))
    plan[9].append(("wo1", 0))
    plan[12].append(("turn_ff", 0))
    plan[14] += [("up", 0), ("up", 1)]
    plan[16].append(("down", 0))
    for n in range(4):
        plan[18 + n // 2 * 2 + av_delay].append(("av0", n))
    plan[22].append(("wo0", 0))
    plan[22].append(("turn_qkv", 0))
    for c in range(NC_H):
        plan[24 + c // 4].append(("qk", c))
    for h in range(H):
        plan[26 + h // 8].append(("dots0", h))
    for n in range(6):
        plan[28 + n // 2].append(("v", n))
    return plan


ADD_WO1, BRING, ADD_DOWN, STATS_QKV, KMEM, ADD_WO0 = 12, 14, 18, 20, 22, 24
PLAN = side_plan(0)
ACT_PLAN = side_plan(2)
FIRST_JOBS = [("turn_qkv", 0)] + [("qk", c) for c in range(NC_H)] + [("dots0", h) for h in range(H)] \
    + [("v", n) for n in range(6)]
LAST_JOBS = [("av1", n) for n in range(4)] + [("wo1", 0), ("turn_ff", 0), ("up", 0), ("up", 1), ("down", 0)]
SIDE_BANKS = 4


def takes_bank(job):
    return not (job[0] in ("av0", "av1") and job[1] % 2)


def program(nc, a, out):
    with ExitStack() as ctx:
        def sb(name, shape, where=None):
            return (where or ctx).enter_context(nc.sbuf_tensor(name, shape, F32))

        def sem(name):
            return ctx.enter_context(nc.semaphore(name))

        x = sb("x", [P, B + 2, TT * D])
        ident = sb("ident", [P, P])
        minus_half = sb("minus_half", [P, TT])
        ones = sb("ones", [1, P])
        mv = sb("mv", [P, 2, TT, 2])
        bst = sb("bst", [P, TT, 6])
        rstd = sb("rstd", [P, 2, TT])
        shift = sb("shift", [P, 2, TT])
        vare = sb("vare", [P, TT])

        s_load = sem("s_load")
        s_set = sem("s_set")
        s_diag = sem("s_diag")
        s_out = sem("s_out")
        s_tail = sem("s_tail")
        s_mask = sem("s_mask")
        banks = [ctx.enter_context(nc.psum_tensor(f"bank{i}", [P, 512], F32)) for i in range(8)]

        attention(nc, a, x, ident, minus_half, ones, mv, bst, rstd, shift, vare, banks, s_load, s_set, s_diag)

        tail(nc, a, x, ident, minus_half, mv, bst, rstd, vare, banks, s_tail, s_mask)
        with nc.Block() as block:
            @block.sync
            def _(sp):
                sp.dma_start(out.rearrange("b (t p) d -> p b t d", p=P),
                             x[:, 1:B + 1, :].rearrange("p b (t d) -> p b t d", t=TT)).then_inc(s_out, 16)
                sp.wait_ge(s_out, 16)


def attention(nc, a, x, ident, minus_half, ones, mv, bst, rstd, shift, vare, banks, s_load, s_set, s_diag):
    with ExitStack() as ctx:
        def sb(name, shape):
            return ctx.enter_context(nc.sbuf_tensor(name, shape, F32))

        sems = []

        def sem(name):
            s = ctx.enter_context(nc.semaphore(name))
            sems.append(s)
            return s

        wq = sb("wq", [P, DEPTH, H * DH])
        wk = sb("wk", [P, DEPTH, H * DH])
        wv = sb("wv", [P, DEPTH, H * DH])
        wo = sb("wo", [P, DEPTH, NC_H, D])
        w1 = sb("w1", [P, DEPTH, FC * P])
        w2 = sb("w2", [P, DEPTH, FC, D])
        gains = sb("gains", [P, 4, DEPTH])
        b1 = sb("b1", [P, DEPTH, FC])
        bo = sb("bo", [1, DEPTH, D])
        b2 = sb("b2", [1, DEPTH, D])
        pre = sb("pre", [P, DEPTH, P])
        post = sb("post", [P, DEPTH, H * ROWS])
        own = sb("own", [P, ROWS])
        stack = sb("stack", [P, 2, DEPTH, H])
        causal = sb("causal", [P, ROWS])

        z = sb("z", [P, 2, TT * D])
        xh = sb("xh", [P, TT * D])
        xnT = sb("xnT", [P, MKV + T])
        qT = sb("qT", [P, NC_H, T])
        kmem = sb("kmem", [P, DEPTH, NC_H, MKV])
        kT = sb("kT", [P, NC_H, J])
        v = sb("v", [P, 2, 3, H * DH])
        dots = [sb(f"dots{i}", [P, H, WI[i]]) for i in range(TT)]
        gathered = sb("gathered", [P, DR, J])
        mixed = sb("mixed", [P, XS, J])
        left = sb("left", [P, 2, J])
        top = sb("top", [P, XS, TOPK])
        nmax = sb("nmax", [P, XS])
        e = sb("e", [P, ES, J])
        total = sb("total", [P, 2])
        rtotal = sb("rtotal", [P, 2])
        spost = sb("spost", [P, 2, H * ROWS])
        pT = [[sb(f"pT{i}{c}", [n, H, P]) for c, (_, n) in enumerate(key_chunks(WI[i]))] for i in range(TT)]
        oT = sb("oT", [P, NC_H, P])
        gT = sb("gT", [P, FC, T])

        mix_bank, post_bank, side_bank = banks[0:2], banks[2:4], banks[4:8]

        with nc.Block() as block:
            @block.sync
            def _(sp):
                loads = [
                    (x[:, 1:3, :].rearrange("p b (t d) -> p b t d", t=TT),
                     a["x"][0:2].rearrange("b (t p) d -> p b t d", p=P)),
                    (x[:, 3:B + 1, :].rearrange("p b (t d) -> p b t d", t=TT),
                     a["x"][2:B].rearrange("b (t p) d -> p b t d", p=P)),
                    (wq[:, :, :], a["wq"].rearrange("l p n -> p l n")),
                    (wk[:, :, :], a["wk"].rearrange("l p n -> p l n")),
                    (wv[:, :, :], a["wv"].rearrange("l p n -> p l n")),
                    (gains[:, :, :], a["gains"]),
                    (b1[:, :, :], a["b1"]),
                    (bo[:, :, :], a["bo"][None, :, :]),
                    (b2[:, :, :], a["b2"][None, :, :]),
                ]
                for l in range(DEPTH):
                    loads.append((wo[:, l, :, :], a["wo"][l].rearrange("(c p) n -> p c n", p=P)))
                    loads.append((w2[:, l, :, :], a["w2"][l].rearrange("(c p) n -> p c n", p=P)))
                    loads.append((w1[:, l, :], a["w1"][l]))
                    for hh in range(2):
                        loads.append((kmem[hh * DH:(hh + 1) * DH, l, :, :],
                                      a["mem_kT"][l].rearrange("(c hh) d m -> hh d c m", hh=2)[hh]))
                for to, source in loads:
                    sp.dma_start(to, source).then_inc(s_load, 16)
                for n, name in enumerate(("pre", "post")):
                    for i in range(ROWS):
                        sp.dma_start(stack[i * H:(i + 1) * H, n, :, :], a[name].rearrange("l h k -> h l k")) \
                          .then_inc(s_diag, 16)
                sp.wait_ge(s_load, 16 * len(loads))
                sp.wait_ge(s_diag, 16 * 2 * ROWS)

            @block.gpsimd
            def _(pool):
                pool.memset(ident[:, :], 0.0).then_inc(s_set, 1)
                pool.memset(own[:, :], 1.0).then_inc(s_set, 1)
                pool.memset(causal[:, :], 0.0).then_inc(s_set, 1)
                pool.memset(ones[:, :], 1.0).then_inc(s_set, 1)
                pool.memset(minus_half[:, :], -0.5).then_inc(s_set, 1)
                pool.wait_ge(s_set, 3)
                pool.affine_select(out=ident[:, :], in_=ident[:, :], compare_op=ALU.not_equal, fill=1.0, base=0,
                                   pattern=[[-1, P]], channel_multiplier=1).then_inc(s_set, 1)
                pool.affine_select(out=causal[:, :], in_=causal[:, :], compare_op=ALU.is_ge, fill=MASKED, base=0,
                                   pattern=[[-H, ROWS]], channel_multiplier=1).then_inc(s_set, 1)
                pool.affine_select(out=own[:, :], in_=own[:, :], compare_op=ALU.is_ge, fill=0.0, base=0,
                                   pattern=[[-H, ROWS]], channel_multiplier=1).then_inc(s_set, 1)
                pool.wait_ge(s_set, 8)
                pool.affine_select(out=own[:, :], in_=own[:, :], compare_op=ALU.is_ge, fill=0.0, base=H - 1,
                                   pattern=[[H, ROWS]], channel_multiplier=-1).then_inc(s_set, 1)

            @block.vector
            def _(dve):
                for buf in (z[:, :, :], xnT[:, 0:MKV], x[:, 0, :], x[:, B + 1, :], v[:, :, :, :]):
                    dve.memset(buf, 0.0)
                for half in pT:
                    for chunk in half:
                        dve.memset(chunk[:, :, :], 0.0)
                dve.wait_ge(s_set, 9)
                dve.wait_ge(s_diag, 16 * 2 * ROWS)
                for l in range(DEPTH):
                    dve.tensor_tensor(pre[:, l, :].rearrange("p (i k) -> p i k", i=ROWS),
                                      stack[:, 0, l, None, :].broadcast_to([P, ROWS, H]),
                                      own[:, :, None].broadcast_to([P, ROWS, H]), ALU.mult)
                    dve.tensor_tensor(post[:, l, :].rearrange("p (k i) -> p k i", i=ROWS),
                                      stack[:, 1, l, :, None].broadcast_to([P, H, ROWS]),
                                      own[:, None, :].broadcast_to([P, H, ROWS]), ALU.mult)

        s_gath = [sem(f"s_gath{i}") for i in range(DR)]
        s_vmem = sem("s_vmem")
        s_kmem = sem("s_kmem")
        s_mix = sem("s_mix")
        s_x = sem("s_x")
        s_masked = sem("s_masked")
        s_max = sem("s_max")
        s_dve = sem("s_dve")
        s_nmax = sem("s_nmax")
        s_e = sem("s_e")
        s_r = sem("s_r")
        s_spost = sem("s_spost")
        s_post = sem("s_post")
        s_p = sem("s_p")
        s_full = [sem(f"s_full{i}") for i in range(SIDE_BANKS)]
        s_free = [sem(f"s_free{i}") for i in range(SIDE_BANKS)]
        s_xin = sem("s_xin")
        s_stats = sem("s_stats")
        s_pool = sem("s_pool")
        s_norm = sem("s_norm")

        def run(jobs_of_steps, ln_order, tiles, x_done, x_new):
            turns = Turns([(s,) + job for s, jobs in jobs_of_steps for job in jobs if takes_bank(job)], SIDE_BANKS)
            now = {s: (s % PAIR) // 2 for s, _ in jobs_of_steps}
            done = {s: ((s - 1) % PAIR) // 2 for s, _ in jobs_of_steps}
            coming = {s: ((s + 1) % PAIR) // 2 for s, _ in jobs_of_steps}

            def acquire(pe, s, job):
                b = turns.bank((s,) + job)
                wait(pe, s_free[b], turns.free((s,) + job))
                return side_bank[b], s_full[b]

            def filled(eng, s, job):
                b = turns.bank((s,) + job)
                eng.wait_ge(s_full[b], turns.full((s,) + job))
                return side_bank[b], s_free[b]

            def emptied(eng, s, job):
                if (s,) + job in turns.at:
                    eng.wait_ge(s_free[turns.bank((s,) + job)], turns.full((s,) + job))

            def vmems(s):
                return sum(1 for r, jobs in jobs_of_steps if ("v", 5) in jobs and r <= s)

            kmems = vmems

            def pool_kmem(pool, s):
                if (s, "dots1", H - 1) in turns.at:
                    filled(pool, s, ("dots1", H - 1))
                pool.tensor_copy(kT[:, :, 0:MKV], kmem[:, coming[s], :, :]).then_inc(s_kmem, 1)

            def sp_vmem(sp, s):
                emptied(sp, s, ("v", 1))
                sp.dma_start(v[0:MKV, (s + 1) % 2, 0, :].rearrange("m (h d) -> m h d", h=H),
                             a["mem_v"][coming[s]].rearrange("h m d -> m h d")).then_inc(s_vmem, 16)

            def norms(s, kind):
                return ln_order.index((s, kind)) + 1

            def pe_dots(pe, s, half, h):
                bank, full = acquire(pe, s, (f"dots{half}", h))
                if h == 0:
                    emptied(pe, s if half == 0 else s - 1, ("qk", NC_H - 1))
                    wait(pe, s_kmem, kmems(s if half == 0 else s - 1))
                lo = DH * (h % 2)
                nc.tensor.matmul(bank[:, 0:WI[half]], qT[lo:lo + DH, h // 2, half * P:(half + 1) * P],
                                 kT[lo:lo + DH, h // 2, 0:WI[half]], start=True, stop=True).then_inc(full, 1)

            def pe_av(pe, s, half, n, stream):
                if n % 2 == 0:
                    acquire(pe, s, (f"av{half}", n))
                b = turns.bank((s, f"av{half}", n - n % 2))
                if n == 0 and tiles:
                    wait(pe, s_p, TILES * s + (HALF if half == 0 else 0))
                if n == 0 and half == 0:
                    emptied(pe, s - 1, ("v", 5))
                    wait(pe, s_vmem, 16 * vmems(s - 1))
                parts = key_chunks(WI[half])
                for pair in range(2 * n, 2 * n + 2):
                    c = pair % 4
                    for k, (j, m) in enumerate(parts):
                        for lo in (0, DH):
                            h = 2 * pair + lo // DH
                            last = nc.tensor.matmul(side_bank[b][lo:lo + DH, c * P:(c + 1) * P],
                                                    v[0:m, stream, k, h * DH:(h + 1) * DH], pT[half][k][0:m, h, :],
                                                    start=(k == 0), stop=(k == len(parts) - 1))
                if n % 2 == 1:
                    last.then_inc(s_full[b], 1)

            def pe_wo(pe, s, half, layer):
                bank, full = acquire(pe, s, (f"wo{half}", 0))
                emptied(pe, s, (f"av{half}", 2))
                for c in range(NC_H):
                    nc.tensor.matmul(bank[:, 0:D], oT[:, c, :], wo[:, layer, c, :], start=(c == 0), stop=False)
                nc.tensor.matmul(bank[:, 0:D], ones[0:1, :], bo[0:1, layer, :], start=False, stop=True) \
                    .then_inc(full, 1)

            def pe_turn(pe, s, name, kind):
                bank, full = acquire(pe, s, (name, 0))
                pe.wait_ge(s_norm, norms(s, kind))
                for t in range(TT):
                    last = nc.tensor.transpose(bank[:, t * P:(t + 1) * P], xh[:, t * D:(t + 1) * D], ident[:, :])
                last.then_inc(full, 1)

            def pe_up(pe, s, n, layer):
                bank, full = acquire(pe, s, ("up", n))
                emptied(pe, s, ("turn_ff", 0))
                for c in range(2):
                    f = (2 * n + c) * P
                    last = nc.tensor.matmul(bank[:, c * T:(c + 1) * T], w1[:, layer, f:f + P], xnT[:, MKV:J],
                                            start=True, stop=True)
                last.then_inc(full, 1)

            def pe_down(pe, s, layer):
                bank, full = acquire(pe, s, ("down", 0))
                emptied(pe, s, ("up", 1))
                for t in range(TT):
                    for c in range(FC):
                        nc.tensor.matmul(bank[:, t * D:(t + 1) * D], gT[:, c, t * P:(t + 1) * P], w2[:, layer, c, :],
                                         start=(c == 0), stop=False)
                    last = nc.tensor.matmul(bank[:, t * D:(t + 1) * D], ones[0:1, :], b2[0:1, layer, :],
                                            start=False, stop=True)
                last.then_inc(full, 1)

            def pe_qk(pe, s, c, layer):
                bank, full = acquire(pe, s, ("qk", c))
                emptied(pe, s, ("turn_qkv", 0))
                nc.tensor.matmul(bank[:, 0:T], wq[:, layer, c * P:(c + 1) * P], xnT[:, MKV:J], start=True, stop=True)
                nc.tensor.matmul(bank[:, T:2 * T], wk[:, layer, c * P:(c + 1) * P], xnT[:, MKV:J],
                                 start=True, stop=True).then_inc(full, 1)

            def pe_v(pe, s, n, layer):
                r, cols = n // 2, slice((n % 2) * 512, (n % 2 + 1) * 512)
                m = min(P, J - r * P)
                bank, full = acquire(pe, s, ("v", n))
                nc.tensor.matmul(bank[0:m, :], xnT[:, r * P:r * P + m], wv[:, layer, cols],
                                 start=True, stop=True).then_inc(full, 1)

            def pe_side(pe, s, name, n):
                if name == "dots1":
                    pe_dots(pe, s, 1, n)
                elif name == "dots0":
                    pe_dots(pe, s, 0, n)
                elif name == "av1":
                    pe_av(pe, s, 1, n, (s - 1) % 2)
                elif name == "av0":
                    pe_av(pe, s, 0, n, s % 2)
                elif name == "wo1":
                    pe_wo(pe, s, 1, done[s])
                elif name == "wo0":
                    pe_wo(pe, s, 0, now[s])
                elif name == "turn_ff":
                    pe_turn(pe, s, name, "ff")
                elif name == "turn_qkv":
                    pe_turn(pe, s, name, "qkv")
                elif name == "up":
                    pe_up(pe, s, n, done[s])
                elif name == "down":
                    pe_down(pe, s, done[s])
                elif name == "qk":
                    pe_qk(pe, s, n, coming[s])
                elif name == "v":
                    pe_v(pe, s, n, coming[s])

            def pe_mix(pe, n):
                w, bank = width(n % TILES), mix_bank[n % 2]
                pe.wait_ge(s_gath[n % DR], 16 * (n // DR + 1))
                wait(pe, s_x, n - 1)
                nc.tensor.matmul(bank[:, 0:w], pre[:, now[n // TILES], :], gathered[:, n % DR, 0:w],
                                 start=True, stop=True).then_inc(s_mix, 1)

            def pe_post(pe, n):
                pe.wait_ge(s_spost, n + 1)
                wait(pe, s_p, n - 1)
                for k, (j, m) in enumerate(key_chunks(width(n % TILES))):
                    last = nc.tensor.matmul(post_bank[n % 2][0:m, k * P:(k + 1) * P], e[:, n % ES, j:j + m],
                                            spost[:, n % 2, :], start=True, stop=True)
                last.then_inc(s_post, 1)

            def act_side(act, s, name, n):
                if name in ("wo0", "wo1", "down") or not takes_bank((name, n + 1)) and n % 2 == 0:
                    return
                if name in ("av0", "av1"):
                    bank, free = filled(act, s, (name, n - 1))
                    act.copy(oT[:, 2 * (n - 1):2 * (n - 1) + 4, :].rearrange("p c i -> p (c i)"), bank[:, :]) \
                       .then_inc(free, 1)
                    return
                bank, free = filled(act, s, (name, n))
                if name in ("dots0", "dots1"):
                    half = int(name[4])
                    act.copy(dots[half][:, n, :], bank[:, 0:WI[half]]).then_inc(free, 1)
                elif name in ("turn_ff", "turn_qkv"):
                    row, layer = (2, done[s]) if name == "turn_ff" else (0, coming[s])
                    act.activation(xnT[:, MKV:J], bank[:, 0:T], ACT.Identity, bias=gains[:, row + 1, layer:layer + 1],
                                   scale=gains[:, row, layer:layer + 1]).then_inc(free, 1)
                elif name == "up":
                    for c in range(2):
                        f = 2 * n + c
                        last = act.activation(gT[:, f, :], bank[:, c * T:(c + 1) * T], ACT.Gelu,
                                              bias=b1[:, done[s], f:f + 1])
                    last.then_inc(free, 1)
                elif name == "qk":
                    act.mul(qT[:, n, :], bank[:, 0:T], float(DH) ** -0.5)
                    act.copy(kT[:, n, MKV:J], bank[:, T:2 * T]).then_inc(free, 1)
                elif name == "v":
                    r, m = n // 2, min(P, J - n // 2 * P)
                    act.copy(v[0:m, (s + 1) % 2, r, (n % 2) * 512:(n % 2 + 1) * 512], bank[0:m, :]).then_inc(free, 1)

            def act_copy(act, n):
                w = width(n % TILES)
                act.wait_ge(s_mix, n + 1)
                wait(act, s_r, n + 1 - XS)
                act.copy(mixed[:, n % XS, 0:w], mix_bank[n % 2][:, 0:w]).then_inc(s_x, 1)

            def act_exp(act, n):
                w = width(n % TILES)
                act.wait_ge(s_nmax, n + 1)
                if w <= TOPK:
                    wait(act, s_r, n - 1)
                    act.activation(e[:, n % ES, 0:w], mixed[:, n % XS, 0:w], ACT.Exp, bias=nmax[:, n % XS:n % XS + 1],
                                   accum_out=total[:, n % 2:n % 2 + 1]).then_inc(s_e, 1)
                else:
                    act.activation(e[:, n % ES, 0:w], mixed[:, n % XS, 0:w], ACT.Exp,
                                   bias=nmax[:, n % XS:n % XS + 1]).then_inc(s_e, 1)

            def act_probs(act, n):
                t = n % TILES
                half, at = t // HALF, ROWS * (t % HALF)
                act.wait_ge(s_post, n + 1)
                for k, (j, m) in enumerate(key_chunks(width(t))):
                    last = act.copy(pT[half][k][0:m, :, at:at + ROWS],
                                    post_bank[n % 2][0:m, k * P:(k + 1) * P].rearrange("p (h i) -> p h i", i=ROWS))
                last.then_inc(s_p, 1)

            chain = [0]

            def link(ins):
                ins.then_inc(s_dve, 1)
                chain[0] += 1
                return chain[0]

            def dve_own(dve):
                dve.wait_ge(s_dve, chain[0])

            late = []

            def dve_inverse(dve, n):
                wait(dve, s_spost, n - 1)
                dve.reciprocal(rtotal[:, n % 2:n % 2 + 1], total[:, n % 2:n % 2 + 1]).then_inc(s_r, 1)

            def dve_top(dve, tiles_at_once):
                w = {n: width(n % TILES) for n in tiles_at_once}
                at = {}
                for n in tiles_at_once:
                    dve.wait_ge(s_masked, n + 1)
                    wait(dve, s_nmax, n + 1 - XS)
                    dve.max(top[:, n % XS, 0:8], mixed[:, n % XS, 0:w[n]]).then_inc(s_max, 1)
                while late:
                    n = late.pop(0)
                    dve.wait_ge(s_e, n + 1)
                    dve_inverse(dve, n)
                picky = [n for n in tiles_at_once if w[n] > TOPK]
                for r in range(8, TOPK, 8):
                    for n in picky:
                        if r == 8:
                            dve.wait_ge(s_max, n + 1)
                        else:
                            dve.wait_ge(s_dve, at[n])
                        source = mixed[:, n % XS, 0:w[n]] if r == 8 else left[:, n % 2, 0:w[n]]
                        at[n] = link(dve.match_replace(left[:, n % 2, 0:w[n]], top[:, n % XS, r - 8:r], source, TAKEN))
                    for n in picky:
                        dve.wait_ge(s_dve, at[n])
                        at[n] = link(dve.max(top[:, n % XS, r:r + 8], left[:, n % 2, 0:w[n]]))
                for n in picky:
                    dve.wait_ge(s_e, n + 1)
                    dve.wait_ge(s_dve, at[n])
                    at[n] = link(dve.scalar_tensor_tensor(
                        out=e[:, n % ES, 0:w[n]], in0=mixed[:, n % XS, 0:w[n]], scalar=top[:, n % XS, TOPK - 1:TOPK],
                        in1=e[:, n % ES, 0:w[n]], op0=ALU.is_ge, op1=ALU.mult, accum_out=total[:, n % 2:n % 2 + 1]))
                for n in tiles_at_once:
                    if n in picky:
                        dve.wait_ge(s_dve, at[n])
                        dve_inverse(dve, n)
                    else:
                        late.append(n)

            def dve_stats(dve, s, kind, source):
                k = norms(s, kind) - 1
                for t in range(TT):
                    link(dve.bn_stats(bst[:, t, :], source[:, t * D:(t + 1) * D]))
                dve_own(dve)
                for t in range(TT):
                    last = dve.bn_aggr(mv[:, k % 2, t, :], bst[:, t, :])
                last.then_inc(s_stats, 1)
                dve.wait_ge(s_stats, k + 1)

            def dve_wo(dve, s, half, stream):
                bank, free = filled(dve, s, (f"wo{half}", 0))
                part = z[:, stream, half * D:(half + 1) * D]
                dve.tensor_tensor(part, part, bank[:, 0:D], ALU.add).then_inc(free, 1)

            def dve_down(dve, s):
                stream = (s - 1) % 2
                bank, free = filled(dve, s, ("down", 0))
                dve.tensor_tensor(z[:, stream, :], z[:, stream, :], bank[:, 0:TT * D], ALU.add).then_inc(free, 1)
                if done[s] == DEPTH - 1:
                    emptied(dve, s, ("down", 0))
                    here = x[:, bass.ds(x_done(s), 1), :]
                    link(dve.tensor_tensor(here, here, z[:, stream:stream + 1, :], ALU.add))

            pooled = [0]

            def pool_link(pool, ins):
                ins.then_inc(s_pool, 1)
                pooled[0] += 1
                pool.wait_ge(s_pool, pooled[0])

            def pool_bring(pool, s):
                if (s, "turn_ff", 0) in turns.at:
                    filled(pool, s, ("turn_ff", 0))
                pool.tensor_copy(xh[:, None, :], x[:, bass.ds(x_new(s), 1), :]).then_inc(s_xin, 1)

            def pool_norm(pool, s, kind, source, to):
                k = norms(s, kind) - 1
                m = mv[:, k % 2, :, :]
                before = {"ff": (s - 1, "turn_qkv", 0), "qkv": (s, "turn_ff", 0)}.get(kind)
                if before in turns.at:
                    filled(pool, before[0], before[1:])
                pool.wait_ge(s_stats, k + 1)
                pool_link(pool, pool.tensor_scalar(vare[:, :], m[:, :, 1], 1.0, EPS, ALU.mult, ALU.add))
                pool_link(pool, pool.tensor_tensor(rstd[:, k % 2, :], vare[:, :], minus_half[:, :], ALU.pow))
                pool_link(pool, pool.tensor_tensor(shift[:, k % 2, :], m[:, :, 0], rstd[:, k % 2, :], ALU.mult))
                for t in range(TT):
                    last = pool.tensor_scalar(to[:, t * D:(t + 1) * D], source[:, t * D:(t + 1) * D],
                                              rstd[:, k % 2, t:t + 1], shift[:, k % 2, t:t + 1], ALU.mult, ALU.subtract)
                last.then_inc(s_norm, 1)
                pool.wait_ge(s_norm, k + 1)

            def pool_nmax(pool, n):
                pool.wait_ge(s_max, n + 1)
                wait(pool, s_e, n + 1 - XS)
                pool.tensor_scalar(nmax[:, n % XS:n % XS + 1], top[:, n % XS, 0:1], -1.0, 1.0, ALU.mult, ALU.mult) \
                    .then_inc(s_nmax, 1)

            def pool_mask(pool, n):
                w = width(n % TILES)
                pool.wait_ge(s_x, n + 1)
                edge = mixed[:, n % XS, w - ROWS:w]
                pool.tensor_tensor(edge, edge, causal[:, :], ALU.add).then_inc(s_masked, 1)

            def pool_spost(pool, n):
                pool.wait_ge(s_r, n + 1)
                wait(pool, s_post, n - 1)
                pool.tensor_scalar(spost[:, n % 2, :], post[:, now[n // TILES], :], rtotal[:, n % 2:n % 2 + 1], 1.0,
                                   ALU.mult, ALU.mult).then_inc(s_spost, 1)

            with nc.Block() as block:
                @block.sync
                def _(sp):
                    if not tiles and ("v", 1) in jobs_of_steps[0][1]:
                        sp_vmem(sp, jobs_of_steps[0][0])
                    for n in range(tiles):
                        s, t = n // TILES, n % TILES
                        if t == 0:
                            emptied(sp, s - 1, ("dots0", H - 1))
                        if t == HALF:
                            emptied(sp, s, ("dots1", H - 1))
                        wait(sp, s_mix, n + 1 - DR)
                        i = ROWS * (t % HALF)
                        if t == 4 and s > 0:
                            sp_vmem(sp, s - 1)
                        sp.dma_start(gathered[:, n % DR, 0:width(t)],
                                     dots[t // HALF][i:i + ROWS, :, 0:width(t)]).then_inc(s_gath[n % DR], 16)

                    if tiles:
                        sp_vmem(sp, STEPS - 1)
                    wait(sp, s_vmem, 16 * vmems(STEPS))

                @block.tensor
                def _(pe):
                    if not tiles:
                        for s, jobs in jobs_of_steps:
                            for name, k in jobs:
                                pe_side(pe, s, name, k)
                        return
                    for n in range(4):
                        pe_mix(pe, n)
                    for n in range(0, tiles, 2):
                        if n:
                            pe_post(pe, n - 2)
                            pe_post(pe, n - 1)
                        if n + 4 < tiles:
                            pe_mix(pe, n + 4)
                            pe_mix(pe, n + 5)
                        for name, k in PLAN[n % TILES] + PLAN[n % TILES + 1]:
                            pe_side(pe, n // TILES, name, k)
                    pe_post(pe, tiles - 2)
                    pe_post(pe, tiles - 1)

                @block.scalar
                def _(act):
                    if not tiles:
                        for s, jobs in jobs_of_steps:
                            for name, k in jobs:
                                act_side(act, s, name, k)
                        return
                    for n in range(4):
                        act_copy(act, n)
                    for n in range(0, tiles, 2):
                        act_exp(act, n)
                        act_exp(act, n + 1)
                        if n:
                            act_probs(act, n - 2)
                            act_probs(act, n - 1)
                        if n + 4 < tiles:
                            act_copy(act, n + 4)
                            act_copy(act, n + 5)
                        for name, k in ACT_PLAN[n % TILES] + ACT_PLAN[n % TILES + 1]:
                            act_side(act, n // TILES, name, k)
                    act_probs(act, tiles - 2)
                    act_probs(act, tiles - 1)

                def dve_finish(dve, s, at=None):
                    if at in (None, ADD_WO1):
                        dve_wo(dve, s, 1, (s - 1) % 2)
                        emptied(dve, s, ("wo1", 0))
                        dve_stats(dve, s, "ff", z[:, (s - 1) % 2, :])
                    if at in (None, ADD_DOWN):
                        dve_down(dve, s)

                def dve_prepare(dve, s, at=None):
                    if at in (None, ADD_DOWN) and (s, "new") in ln_order:
                        dve.wait_ge(s_xin, sum(1 for r, kind in ln_order if kind == "new" and r <= s))
                        dve_stats(dve, s, "new", xh)
                    if at in (None, STATS_QKV):
                        if (s, "new") in ln_order:
                            dve.wait_ge(s_norm, norms(s, "new"))
                        dve_stats(dve, s, "qkv", z[:, (s + 1) % 2, :])

                @block.vector
                def _(dve):
                    for s, jobs in jobs_of_steps:
                        if not tiles:
                            if ("wo1", 0) in jobs:
                                dve_finish(dve, s)
                            else:
                                dve_prepare(dve, s)
                            continue
                        for t in range(0, TILES, 2):
                            dve_finish(dve, s, t)
                            dve_prepare(dve, s, t)
                            if t == ADD_WO0:
                                dve_wo(dve, s, 0, s % 2)
                            dve_top(dve, (TILES * s + t, TILES * s + t + 1))

                def pool_finish(pool, s, at=None):
                    if at in (None, ADD_WO1):
                        pool_norm(pool, s, "ff", z[:, (s - 1) % 2, :], xh)

                def pool_prepare(pool, s, at=None):
                    if (s, "new") in ln_order:
                        if at in (None, BRING):
                            pool_bring(pool, s)
                        if at in (None, ADD_DOWN):
                            pool_norm(pool, s, "new", xh, z[:, (s + 1) % 2, :])
                    if at in (None, STATS_QKV):
                        pool_norm(pool, s, "qkv", z[:, (s + 1) % 2, :], xh)
                    if at in (None, KMEM):
                        pool_kmem(pool, s)

                @block.gpsimd
                def _(pool):
                    if tiles:
                        for n in range(4):
                            pool_mask(pool, n)
                    for s, jobs in jobs_of_steps:
                        if not tiles:
                            if ("wo1", 0) in jobs:
                                pool_finish(pool, s)
                            else:
                                pool_prepare(pool, s)
                            continue
                        for t in range(0, TILES, 2):
                            n = TILES * s + t
                            if n:
                                pool_spost(pool, n - 2)
                                pool_spost(pool, n - 1)
                            pool_nmax(pool, n)
                            pool_nmax(pool, n + 1)
                            if n + 4 < tiles:
                                pool_mask(pool, n + 4)
                                pool_mask(pool, n + 5)
                            pool_finish(pool, s, t)
                            pool_prepare(pool, s, t)
                    if tiles:
                        pool_spost(pool, tiles - 2)
                        pool_spost(pool, tiles - 1)

            for used in sems:
                nc.sync.sem_clear(used)
            nc.all_engine_barrier(sem_only=True)

        run([(-1, FIRST_JOBS)], [(-1, "new"), (-1, "qkv")], 0, None, lambda s: 1)
        step_jobs = [job for t in range(TILES) for job in PLAN[t]]
        order = [(first + s, kind) for first in range(0, STEPS, PAIR)
                 for s, kind in ((0, "ff"), (0, "new"), (0, "qkv"), (1, "ff"), (1, "qkv"), (2, "ff"), (2, "qkv"),
                                 (3, "ff"), (3, "new"), (3, "qkv"))]
        with nc.Fori(0, B * PAIR // (2 * STEPS)) as turn:
            def slot(s):
                return turn * (2 * STEPS // PAIR) + (2 * (s // PAIR) + {0: 0, 3: 1}[s % PAIR])

            run([(s, step_jobs) for s in range(STEPS)], order, TILES * STEPS, slot, lambda s: slot(s) + 2)
        run([(STEPS, LAST_JOBS)], [(STEPS, "ff")], 0, lambda s: B, None)


EXPERTS, HIDDEN = 8, 512
CAPACITY = int(T * 2.0 / EXPERTS) + 1
HC = HIDDEN // P
GROUP = 8
LH, LD = 16, D // 16
LGROUP = 8
ROWG = 4
PAD = ROWG * LD + LD
LEPS = 1e-6


class Tail:

    def __init__(self, nc, ctx, x, ident, minus_half, mv, bst, rstd, vare):
        self.nc, self.x, self.ident, self.minus_half = nc, x, ident, minus_half
        self.mv, self.bst, self.rstd, self.vare = mv, bst, rstd, vare
        self.xh = ctx.enter_context(nc.sbuf_tensor("xh2", [P, 2, TT * D], F32))
        self.xnT = ctx.enter_context(nc.sbuf_tensor("xnT2", [P, 2, T], F32))
        names = ("s_agg", "s_stat", "s_vare", "s_rstd", "s_tok", "s_turned", "s_xnT")
        self.sems = [ctx.enter_context(nc.semaphore(name)) for name in names]
        self.agg, self.stat, self.var, self.rs, self.tok, self.turned, self.done = self.sems

    def dve_stats(self, dve, i, slot):
        wait(dve, self.stat, i)
        for t in range(TT):
            last = dve.bn_stats(self.bst[:, t, :], self.x[:, bass.ds(slot, 1), t * D:(t + 1) * D]
                                .rearrange("p o d -> p (o d)"))
        last.then_inc(self.agg, 1)
        dve.wait_ge(self.agg, i + 1)
        wait(dve, self.rs, i - 1)
        for t in range(TT):
            last = dve.bn_aggr(self.mv[:, i % 2, t, :], self.bst[:, t, :])
        last.then_inc(self.stat, 1)

    def pool_rstd(self, pool, i):
        pool.wait_ge(self.stat, i + 1)
        pool.tensor_scalar(self.vare[:, :], self.mv[:, i % 2, :, 1], 1.0, EPS, ALU.mult, ALU.add) \
            .then_inc(self.var, 1)
        pool.wait_ge(self.var, i + 1)
        wait(pool, self.tok, i - 1)
        pool.tensor_tensor(self.rstd[:, i % 2, :], self.vare[:, :], self.minus_half[:, :], ALU.pow) \
            .then_inc(self.rs, 1)
        pool.wait_ge(self.rs, i + 1)

    def dve_norm(self, dve, i, slot):
        dve.wait_ge(self.rs, i + 1)
        dve.wait_ge(self.stat, i + 1)
        wait(dve, self.turned, i - 1)
        for t in range(TT):
            last = dve.tensor_scalar(self.xh[:, i % 2, t * D:(t + 1) * D],
                                     self.x[:, bass.ds(slot, 1), t * D:(t + 1) * D].rearrange("p o d -> p (o d)"),
                                     self.mv[:, i % 2, t, 0:1], self.rstd[:, i % 2, t:t + 1],
                                     ALU.subtract, ALU.mult)
        last.then_inc(self.tok, 1)

    def pe_turn(self, pe, i, bank):
        pe.wait_ge(self.tok, i + 1)
        wait(pe, self.done, i - 1)
        for t in range(TT):
            last = pe.transpose(bank[:, t * P:(t + 1) * P], self.xh[:, i % 2, t * D:(t + 1) * D], self.ident[:, :])
        last.then_inc(self.turned, 1)

    def act_turn(self, act, i, bank, readers):
        act.wait_ge(self.turned, i + 1)
        for s, per in readers:
            wait(act, s, per * (i - 1))
        act.copy(self.xnT[:, i % 2, :], bank[:, 0:T]).then_inc(self.done, 1)


def clear(nc, sems):
    for used in sems:
        nc.sync.sem_clear(used)
    nc.all_engine_barrier(sem_only=True)


class Experts:

    def __init__(self, nc, a, ctx):
        def sb(name, shape):
            return ctx.enter_context(nc.sbuf_tensor(name, shape, F32))

        self.router = sb("router", [P, EXPERTS])
        self.w1 = sb("ew1", [P, EXPERTS, HIDDEN])
        self.w2 = sb("ew2", [P, EXPERTS, HC, D])
        self.b1 = sb("eb1", [P, EXPERTS, HC])
        self.b2 = sb("eb2", [EXPERTS, D])
        self.loads = [(self.router[:, :], a["router"]), (self.b1[:, :, :], a["eb1"]), (self.b2[:, :], a["eb2"])]
        for n in range(EXPERTS):
            self.loads.append((self.w1[:, n, :], a["ew1"][n]))
            self.loads.append((self.w2[:, n, :, :], a["ew2"][n].rearrange("(c p) n -> p c n", p=P)))
        self.xall = sb("xall", [P, B, T])
        self.score = sb("score", [P, TT, B, EXPERTS])
        self.one = sb("one_each", [P, TT, B])
        self.inv = sb("inv_each", [P, TT, B])
        self.turned = sb("sturn", [P, T])
        self.left = sb("sleft", [P, T])
        self.top = sb("stop", [P, -(-CAPACITY // 8) * 8])
        self.above = sb("above", [P, T])
        self.equal = sb("equal", [P, T])
        self.run_of = sb("run_of", [P, T])
        self.unit = sb("unit", [P, T])
        self.count = sb("count", [P, 1])
        self.room = sb("room", [P, 1])
        self.gate = sb("gate", [P, TT, B, EXPERTS])
        self.g = sb("g", [P, 2, TT, EXPERTS])
        self.gT = sb("gT8", [EXPERTS, 2, T])
        self.xs = sb("xs", [P, 2, T])
        self.hT = sb("hT", [P, 2, HC, T])
        self.acc = sb("eacc", [P, 2, TT * D])
        names = ("s_logit", "s_score", "s_xall", "s_link", "s_exp", "s_pe", "s_act", "s_g", "s_gt", "s_gT", "s_bias",
                 "s_init", "s_xs", "s_up", "s_h", "s_down", "s_acc", "s_unit")
        self.sem = {name: ctx.enter_context(nc.semaphore("e" + name)) for name in names}

    def route(self, nc, f, banks):
        s = self.sem
        turn_bank, logit_bank = banks[0:2], banks[2:4]
        with nc.Fori(0, B // GROUP) as group:
            with nc.Block() as block:
                def pool_keep(pool, i):
                    pool.wait_ge(f.done, i + 1)
                    pool.tensor_copy(self.xall[:, bass.ds(group * GROUP + i, 1), :], f.xnT[:, i % 2, None, :]) \
                        .then_inc(s["s_xall"], 1)

                @block.vector
                def _(dve):
                    f.dve_stats(dve, 0, group * GROUP + 1)
                    for i in range(GROUP):
                        if i + 1 < GROUP:
                            f.dve_stats(dve, i + 1, group * GROUP + i + 2)
                        f.dve_norm(dve, i, group * GROUP + i + 1)

                @block.gpsimd
                def _(pool):
                    for i in range(GROUP):
                        f.pool_rstd(pool, i)
                        if i:
                            pool_keep(pool, i - 1)
                    pool_keep(pool, GROUP - 1)

                @block.tensor
                def _(pe):
                    f.pe_turn(pe, 0, turn_bank[0])
                    for i in range(GROUP):
                        if i + 1 < GROUP:
                            f.pe_turn(pe, i + 1, turn_bank[(i + 1) % 2])
                        pe.wait_ge(f.done, i + 1)
                        wait(pe, s["s_score"], i - 1)
                        for t in range(TT):
                            last = pe.matmul(logit_bank[i % 2][:, t * EXPERTS:(t + 1) * EXPERTS],
                                             f.xnT[:, i % 2, t * P:(t + 1) * P], self.router[:, :],
                                             start=True, stop=True)
                        last.then_inc(s["s_logit"], 1)

                @block.scalar
                def _(act):
                    for i in range(GROUP):
                        f.act_turn(act, i, turn_bank[i % 2], [(s["s_logit"], 1), (s["s_xall"], 1)])
                        act.wait_ge(s["s_logit"], i + 1)
                        act.copy(self.score[:, :, bass.ds(group * GROUP + i, 1), :],
                                 logit_bank[i % 2][:, 0:TT * EXPERTS]
                                 .rearrange("p (t o e) -> p t o e", t=TT, o=1)).then_inc(s["s_score"], 1)
            clear(nc, f.sems + list(s.values()))

    def choose(self, nc, f, banks):
        s = self.sem
        flat = [P, TT * B, EXPERTS]
        score = self.score[:, :, :, :].rearrange("p t b e -> p (t b) e")
        one = self.one[:, :, :].rearrange("p t b -> p (t b)")
        inv = self.inv[:, :, :].rearrange("p t b -> p (t b)")
        with nc.Block() as block:
            @block.vector
            def _(dve):
                count = [0]

                def link(ins):
                    ins.then_inc(s["s_link"], 1)
                    count[0] += 1
                    dve.wait_ge(s["s_link"], count[0])

                link(dve.memset(self.unit[:, :], 1.0))
                link(dve.tensor_reduce(one, score, mybir.AxisListType.X, ALU.max))
                dve.tensor_tensor(score, score, one[:, :, None].broadcast_to(flat), ALU.subtract) \
                   .then_inc(s["s_unit"], 1)
                dve.wait_ge(s["s_exp"], 1)
                link(dve.tensor_reduce(one, score, mybir.AxisListType.X, ALU.add))
                link(dve.reciprocal(inv, one))
                dve.tensor_tensor(score, score, inv[:, :, None].broadcast_to(flat), ALU.mult) \
                   .then_inc(s["s_unit"], 1)
                dve.wait_ge(s["s_act"], 1)
                source = self.turned[:, :]
                for r in range(0, CAPACITY, 8):
                    link(dve.max(self.top[:, r:r + 8], source))
                    if r + 8 < CAPACITY:
                        link(dve.match_replace(self.left[:, :], self.top[:, r:r + 8], source, TAKEN))
                        source = self.left[:, :]
                last = self.top[:, CAPACITY - 1:CAPACITY]
                link(dve.tensor_scalar(self.above[:, :], self.turned[:, :], last, None, ALU.is_gt, ALU.add,
                                       accum_out=self.count[:, :]))
                link(dve.tensor_scalar(self.equal[:, :], self.turned[:, :], last, None, ALU.is_equal))
                link(dve.tensor_scalar(self.room[:, :], self.count[:, :], -1.0, float(CAPACITY), ALU.mult, ALU.add))
                link(dve.tensor_tensor_scan(self.run_of[:, :], self.unit[:, :], self.equal[:, :], 0.0,
                                            ALU.mult, ALU.add))
                link(dve.scalar_tensor_tensor(out=self.equal[:, :], in0=self.run_of[:, :], scalar=self.room[:, :],
                                              in1=self.equal[:, :], op0=ALU.is_le, op1=ALU.mult))
                link(dve.tensor_tensor(self.above[:, :], self.above[:, :], self.equal[:, :], ALU.add))
                dve.tensor_tensor(self.turned[:, :], self.turned[:, :], self.above[:, :], ALU.mult) \
                   .then_inc(s["s_unit"], 1)

            @block.scalar
            def _(act):
                act.wait_ge(s["s_unit"], 1)
                act.activation(score, score, ACT.Exp).then_inc(s["s_exp"], 1)
                act.wait_ge(s["s_pe"], 1)
                act.copy(self.turned[:, :], banks[0][:, 0:T]).then_inc(s["s_act"], 1)
                act.wait_ge(s["s_pe"], 2)
                act.copy(self.gate[:, :, :, :].rearrange("p t b e -> p (t b e)"), banks[1][:, 0:T]) \
                   .then_inc(s["s_act"], 1)

            @block.tensor
            def _(pe):
                pe.wait_ge(s["s_unit"], 2)
                for t in range(TT):
                    last = pe.transpose(banks[0][:, t * P:(t + 1) * P],
                                        self.score[:, t, :, :].rearrange("p b e -> p (b e)"), f.ident[:, :])
                last.then_inc(s["s_pe"], 1)
                pe.wait_ge(s["s_unit"], 3)
                for t in range(TT):
                    last = pe.transpose(banks[1][:, t * P:(t + 1) * P], self.turned[:, t * P:(t + 1) * P],
                                        f.ident[:, :])
                last.then_inc(s["s_pe"], 1)
        clear(nc, list(s.values()))

    def mix(self, nc, f, banks):
        s = self.sem
        up_bank, down_bank, turn_bank, bias_bank = banks[0:4], banks[4:6], banks[6], banks[7]
        last_k = GROUP * EXPERTS - 1

        with nc.Fori(0, B // GROUP) as group:
            def prepare(eng, stage, i):
                if stage == "gates":
                    eng.tensor_copy(self.g[:, i % 2, :, :].rearrange("p t (o e) -> p t o e", o=1),
                                    self.gate[:, :, bass.ds(group * GROUP + i, 1), :]).then_inc(s["s_g"], 1)
                elif stage == "turn":
                    eng.wait_ge(s["s_g"], i + 1)
                    wait(eng, s["s_gT"], i)
                    for t in range(TT):
                        last = eng.transpose(turn_bank[0:EXPERTS, t * P:(t + 1) * P], self.g[:, i % 2, t, :],
                                             f.ident[:, :])
                    last.then_inc(s["s_gt"], 1)
                elif stage == "copy":
                    eng.wait_ge(s["s_gt"], i + 1)
                    eng.copy(self.gT[:, i % 2, :], turn_bank[0:EXPERTS, 0:T]).then_inc(s["s_gT"], 1)
                elif stage == "bias":
                    eng.wait_ge(s["s_gT"], i + 1)
                    wait(eng, s["s_init"], i)
                    for t in range(TT):
                        last = eng.matmul(bias_bank[:, t * D:(t + 1) * D], self.gT[:, i % 2, t * P:(t + 1) * P],
                                          self.b2[:, :], start=True, stop=True)
                    last.then_inc(s["s_bias"], 1)
                elif stage == "start":
                    eng.wait_ge(s["s_bias"], i + 1)
                    eng.tensor_tensor(self.acc[:, i % 2, None, :], bias_bank[:, None, 0:TT * D],
                                      f.x[:, bass.ds(group * GROUP + i + 1, 1), :], ALU.add).then_inc(s["s_init"], 1)

            def pe_up(pe, k):
                i, n = k // EXPERTS, k % EXPERTS
                if n == 0:
                    pe.wait_ge(s["s_xs"], i + 1)
                for half in range(2):
                    wait(pe, s["s_h"], 2 * k + half - 3)
                    for c in range(2):
                        h = (2 * half + c) * P
                        last = pe.matmul(up_bank[(2 * k + half) % 4][:, c * T:(c + 1) * T],
                                         self.w1[:, n, h:h + P], self.xs[:, i % 2, :], start=True, stop=True)
                    last.then_inc(s["s_up"], 1)

            with nc.Block() as block:
                @block.gpsimd
                def _(pool):
                    for i in range(GROUP):
                        wait(pool, s["s_up"], 2 * EXPERTS * (i - 1))
                        pool.tensor_copy(self.xs[:, i % 2, None, :], self.xall[:, bass.ds(group * GROUP + i, 1), :]) \
                            .then_inc(s["s_xs"], 1)

                @block.tensor
                def _(pe):
                    prepare(pe, "turn", 0)
                    pe_up(pe, 0)
                    prepare(pe, "bias", 0)
                    for k in range(last_k + 1):
                        i, n = k // EXPERTS, k % EXPERTS
                        if k < last_k:
                            pe_up(pe, k + 1)
                        pe.wait_ge(s["s_h"], 2 * k + 2)
                        wait(pe, s["s_acc"], k - 1)
                        for t in range(TT):
                            for c in range(HC):
                                last = pe.matmul(down_bank[k % 2][:, t * D:(t + 1) * D],
                                                 self.hT[:, k % 2, c, t * P:(t + 1) * P], self.w2[:, n, c, :],
                                                 start=(c == 0), stop=(c == HC - 1))
                        last.then_inc(s["s_down"], 1)
                        if i + 1 < GROUP and n == 3:
                            prepare(pe, "turn", i + 1)
                        if i + 1 < GROUP and n == 5:
                            prepare(pe, "bias", i + 1)

                @block.scalar
                def _(act):
                    prepare(act, "copy", 0)
                    for k in range(last_k + 1):
                        i, n = k // EXPERTS, k % EXPERTS
                        wait(act, s["s_down"], k - 1)
                        for half in range(2):
                            act.wait_ge(s["s_up"], 2 * k + half + 1)
                            for c in range(2):
                                h = 2 * half + c
                                last = act.activation(self.hT[:, k % 2, h, :],
                                                      up_bank[(2 * k + half) % 4][:, c * T:(c + 1) * T],
                                                      ACT.Gelu, bias=self.b1[:, n, h:h + 1])
                            last.then_inc(s["s_h"], 1)
                        if i + 1 < GROUP and n == 4:
                            prepare(act, "copy", i + 1)

                @block.vector
                def _(dve):
                    prepare(dve, "gates", 0)
                    prepare(dve, "start", 0)
                    for k in range(last_k + 1):
                        i, n = k // EXPERTS, k % EXPERTS
                        if i + 1 < GROUP and n == 2:
                            prepare(dve, "gates", i + 1)
                        dve.wait_ge(s["s_down"], k + 1)
                        dve.wait_ge(s["s_init"], i + 1)
                        wait(dve, s["s_acc"], k)
                        for t in range(TT):
                            part = self.acc[:, i % 2, t * D:(t + 1) * D]
                            to = part if n < EXPERTS - 1 else \
                                f.x[:, bass.ds(group * GROUP + i + 1, 1), t * D:(t + 1) * D] \
                                .rearrange("p o d -> p (o d)")
                            last = dve.scalar_tensor_tensor(out=to, in0=down_bank[k % 2][:, t * D:(t + 1) * D],
                                                            scalar=self.g[:, i % 2, t, n:n + 1], in1=part,
                                                            op0=ALU.mult, op1=ALU.add)
                        last.then_inc(s["s_acc"], 1)
                        if i + 1 < GROUP and n == 6:
                            prepare(dve, "start", i + 1)
            clear(nc, list(s.values()))

    def run(self, nc, f, banks):
        self.route(nc, f, banks)
        self.choose(nc, f, banks)
        self.mix(nc, f, banks)


class Linear:

    def __init__(self, nc, a, ctx):
        def sb(name, shape):
            return ctx.enter_context(nc.sbuf_tensor(name, shape, F32))

        self.wT = sb("lwT", [P, 5, D])
        self.nbg = sb("nbg", [P, 1])
        self.loads = [(self.wT[:, n, :], a[name]) for n, name in enumerate(("lq", "lk", "lg", "lv", "lo"))]
        self.loads.append((self.nbg[:, :], a["lbg"]))
        self.head = sb("lhead", [P, LH])
        self.fourth = sb("lfourth", [P, ROWG])
        self.tri = sb("ltri", [P, P])
        self.ones = sb("lones", [P, D])
        self.pick = sb("lpick", [P, ROWG * PAD])
        self.mag = sb("lmag", [P, 2, 2 * T])
        self.soft = sb("lsoft", [P, 2, 2 * T])
        self.sig = sb("lsig", [P, 2, T])
        self.qf = sb("lqf", [P, 3, T])
        self.qx = sb("lqx", [P, 2, ROWG, T])
        self.vx = sb("lvx", [P, 3, TT, LH // ROWG, ROWG * PAD])
        self.kf = sb("lkf", [P, 2, P])
        self.state = sb("lstate", [P, 2, 2, D])
        self.s = sb("ls", [P, 2, TT, LH // ROWG, ROWG, P])
        self.den = sb("lden", [P, T])
        self.oT = sb("loT", [P, 2, T])
        names = ("s_proj", "s_mag", "s_soft", "s_eg", "s_v", "s_qf", "s_qx", "s_kt", "s_kf", "s_st", "s_state",
                 "s_sc", "s_s", "s_o", "s_out", "s_y", "s_x", "s_link")
        self.sem = {name: ctx.enter_context(nc.semaphore("l" + name)) for name in names}

    @staticmethod
    def own_columns(padded):
        return padded.rearrange("p (m k) -> p m k", k=PAD)[:, :, 0:LD]

    def run(self, nc, f, banks):
        s = self.sem
        qk_bank, gv_bank, misc, nd_bank, y_bank, s_bank = banks[0], banks[1], banks[2], banks[3], banks[4], banks[5:8]
        rows = LH // ROWG
        per = TT * rows
        with nc.Fori(0, B // LGROUP) as group:
            with nc.Block() as block:
                def slot(i):
                    return group * LGROUP + i + 1

                def pe_project(pe, i):
                    wait(pe, s["s_v"], i)
                    f.pe_turn(pe, i, gv_bank)
                    pe.wait_ge(f.done, i + 1)
                    wait(pe, s["s_soft"], i)
                    for n in range(2):
                        last = pe.matmul(qk_bank[:, n * T:(n + 1) * T], self.wT[:, n, :], f.xnT[:, i % 2, :],
                                         start=True, stop=True)
                    last.then_inc(s["s_proj"], 1)
                    pe.matmul(gv_bank[:, 0:T], self.wT[:, 2, :], f.xnT[:, i % 2, :], start=True, stop=True)
                    for t in range(TT):
                        last = pe.matmul(gv_bank[:, T + t * D:T + (t + 1) * D], f.xnT[:, i % 2, t * P:(t + 1) * P],
                                         self.wT[:, 3, :], start=True, stop=True)
                    last.then_inc(s["s_proj"], 1)

                def pe_scores(pe, i):
                    pe.wait_ge(s["s_soft"], i + 1)
                    wait(pe, s["s_state"], i)
                    pe.transpose(misc[:, 0:P], self.soft[:, i % 2, T:T + P], f.ident[:, :]) \
                      .then_inc(s["s_kt"], 1)
                    pe.wait_ge(s["s_qx"], i + 1)
                    for t in range(TT):
                        for r in range(rows):
                            q = i * per + t * rows + r
                            wait(pe, s["s_s"], q + 1 - len(s_bank))
                            lo = r * ROWG * LD
                            pe.matmul(s_bank[q % len(s_bank)][:, :],
                                      self.soft[lo:lo + ROWG * LD, i % 2, T + t * P:T + (t + 1) * P],
                                      self.qx[lo:lo + ROWG * LD, i % 2, :, t * P:(t + 1) * P],
                                      start=True, stop=True).then_inc(s["s_sc"], 1)
                    pe.wait_ge(s["s_kf"], i + 1)
                    pe.wait_ge(s["s_v"], i + 1)
                    for r in range(rows):
                        pe.matmul(misc[:, r * ROWG * LD:(r + 1) * ROWG * LD], self.kf[:, i % 2, :],
                                  self.own_columns(self.vx[:, i % 3, 0, r, :]), start=True, stop=True)
                    pe.matmul(misc[:, D:2 * D], self.kf[:, i % 2, :], self.ones[:, :], start=True, stop=True) \
                      .then_inc(s["s_st"], 1)

                def pe_values(pe, i):
                    pe.wait_ge(s["s_state"], i + 1)
                    wait(pe, s["s_out"], i)
                    for t in range(TT):
                        pe.wait_ge(s["s_s"], i * per + (t + 1) * rows)
                        for part in range(2):
                            at = part * T + t * P
                            if t:
                                pe.matmul(nd_bank[:, at:at + P], self.state[:, i % 2, part, :],
                                          self.qf[:, i % 3, t * P:(t + 1) * P], start=True, stop=True)
                            for m in range(ROWG):
                                for r in range(rows):
                                    lo, cut = r * ROWG * LD, slice(m * ROWG * LD, (m + 1) * ROWG * LD)
                                    last = pe.matmul(nd_bank[lo:lo + ROWG * LD, at:at + P],
                                                     self.pick[:, cut] if part else self.vx[:, i % 3, t, r, cut],
                                                     self.s[:, i % 2, t, r, m, :], start=(t == 0 and m == 0),
                                                     stop=(t > 0 or m == ROWG - 1), skip_group_check=(t > 0))
                    last.then_inc(s["s_o"], 1)

                def pe_out(pe, i):
                    pe.wait_ge(s["s_out"], i + 1)
                    wait(pe, s["s_x"], i)
                    for t in range(TT):
                        last = pe.matmul(y_bank[:, t * D:(t + 1) * D], self.oT[:, i % 2, t * P:(t + 1) * P],
                                         self.wT[:, 4, :], start=True, stop=True)
                    last.then_inc(s["s_y"], 1)

                @block.tensor
                def _(pe):
                    pe_project(pe, 0)
                    pe_project(pe, 1)
                    pe_scores(pe, 0)
                    for i in range(LGROUP):
                        if i + 2 < LGROUP:
                            pe_project(pe, i + 2)
                        if i + 1 < LGROUP:
                            pe_scores(pe, i + 1)
                        if i:
                            pe_out(pe, i - 1)
                        pe_values(pe, i)
                    pe_out(pe, LGROUP - 1)

                def act_project(act, i):
                    f.act_turn(act, i, gv_bank, [(s["s_proj"], 2)])
                    act.wait_ge(s["s_proj"], 2 * i + 1)
                    wait(act, s["s_soft"], i - 1)
                    act.activation(self.mag[:, i % 2, :], qk_bank[:, :], ACT.Abs).then_inc(s["s_mag"], 1)
                    act.wait_ge(s["s_mag"], 3 * i + 1)
                    act.activation(self.mag[:, i % 2, :], self.mag[:, i % 2, :], ACT.Exp, scale=-1.0) \
                       .then_inc(s["s_mag"], 1)
                    act.wait_ge(s["s_proj"], 2 * i + 2)
                    wait(act, s["s_qf"], i - 1)
                    act.activation(self.sig[:, i % 2, :], gv_bank[:, 0:T], ACT.Exp, bias=self.nbg[:, :], scale=-1.0) \
                       .then_inc(s["s_eg"], 1)
                    act.wait_ge(s["s_mag"], 3 * i + 2)
                    act.activation(self.mag[:, i % 2, :], self.mag[:, i % 2, :], ACT.Ln, bias=1.0) \
                       .then_inc(s["s_mag"], 1)
                    wait(act, s["s_o"], i - 2)
                    for t in range(TT):
                        last = act.copy(self.own_columns(self.vx[:, i % 3, t, :, :].rearrange("p r k -> p (r k)")),
                                        gv_bank[:, T + t * D:T + (t + 1) * D].rearrange("p (h v) -> p h v", v=LD))
                    last.then_inc(s["s_v"], 1)

                def act_keys(act, i):
                    act.wait_ge(s["s_kt"], i + 1)
                    act.copy(self.kf[:, i % 2, :], misc[:, 0:P]).then_inc(s["s_kf"], 1)

                @block.scalar
                def _(act):
                    act_project(act, 0)
                    act_project(act, 1)
                    act_keys(act, 0)
                    for i in range(LGROUP):
                        if i + 2 < LGROUP:
                            act_project(act, i + 2)
                        if i + 1 < LGROUP:
                            act_keys(act, i + 1)

                def pool_heads(pool, i):
                    pool.wait_ge(s["s_qf"], i + 1)
                    wait(pool, s["s_sc"], per * (i - 1))
                    for m in range(ROWG):
                        last = pool.tensor_scalar(self.qx[:, i % 2, m, :], self.qf[:, i % 3, :],
                                                  self.fourth[:, m:m + 1], 1.0, ALU.mult, ALU.mult)
                    last.then_inc(s["s_qx"], 1)

                @block.gpsimd
                def _(pool):
                    f.pool_rstd(pool, 0)
                    f.pool_rstd(pool, 1)
                    pool_heads(pool, 0)
                    for i in range(2, LGROUP + 1):
                        if i < LGROUP:
                            f.pool_rstd(pool, i)
                        pool_heads(pool, i - 1)

                linked = [0]

                def own(dve, ins):
                    ins.then_inc(s["s_link"], 1)
                    linked[0] += 1
                    dve.wait_ge(s["s_link"], linked[0])

                def dve_features(dve, i):
                    dve.wait_ge(s["s_mag"], 3 * i + 3)
                    wait(dve, s["s_sc"], per * (i - 1))
                    dve.scalar_tensor_tensor(out=self.soft[:, i % 2, :], in0=qk_bank[:, :], scalar=0.0,
                                             in1=self.mag[:, i % 2, :], op0=ALU.max, op1=ALU.add) \
                       .then_inc(s["s_soft"], 1)
                    dve.wait_ge(s["s_eg"], i + 1)
                    sig = self.sig[:, i % 2, :]
                    own(dve, dve.tensor_scalar(sig, sig, 1.0, None, ALU.add))
                    own(dve, dve.reciprocal(sig, sig))
                    dve.wait_ge(s["s_soft"], i + 1)
                    wait(dve, s["s_o"], i - 2)
                    dve.scalar_tensor_tensor(out=self.qf[:, i % 3, :], in0=sig, scalar=LEPS,
                                             in1=self.soft[:, i % 2, 0:T], op0=ALU.add, op1=ALU.mult) \
                       .then_inc(s["s_qf"], 1)

                def dve_scores(dve, i):
                    wait(dve, s["s_o"], i - 1)
                    for t in range(TT):
                        for r in range(rows):
                            q = i * per + t * rows + r
                            dve.wait_ge(s["s_sc"], q + 1)
                            dve.tensor_tensor(self.s[:, i % 2, t, r, :, :],
                                              s_bank[q % len(s_bank)][:, :].rearrange("p (m t) -> p m t", m=ROWG),
                                              self.tri[:, None, :].broadcast_to([P, ROWG, P]), ALU.mult) \
                               .then_inc(s["s_s"], 1)
                    dve.wait_ge(s["s_st"], i + 1)
                    for part in range(2):
                        last = dve.tensor_tensor(
                            self.state[:, i % 2, part, :].rearrange("p (h v) -> p h v", v=LD),
                            misc[:, part * D:(part + 1) * D].rearrange("p (h v) -> p h v", v=LD),
                            self.head[:, :, None].broadcast_to([P, LH, LD]), ALU.mult)
                    last.then_inc(s["s_state"], 1)

                def dve_out(dve, i):
                    dve.wait_ge(s["s_o"], i + 1)
                    wait(dve, s["s_out"], i)
                    own(dve, dve.tensor_scalar(self.den[:, :], nd_bank[:, T:2 * T], LEPS, None, ALU.add))
                    own(dve, dve.reciprocal(self.den[:, :], self.den[:, :]))
                    wait(dve, s["s_y"], i - 1)
                    dve.tensor_tensor(self.oT[:, i % 2, :], nd_bank[:, 0:T], self.den[:, :], ALU.mult) \
                       .then_inc(s["s_out"], 1)

                def dve_add(dve, i):
                    dve.wait_ge(s["s_y"], i + 1)
                    here = f.x[:, bass.ds(slot(i), 1), :]
                    dve.tensor_tensor(here, here, y_bank[:, None, 0:TT * D], ALU.add).then_inc(s["s_x"], 1)

                def dve_tokens(dve, i):
                    f.dve_stats(dve, i, slot(i))
                    f.dve_norm(dve, i, slot(i))

                @block.vector
                def _(dve):
                    dve_tokens(dve, 0)
                    dve_tokens(dve, 1)
                    dve_features(dve, 0)
                    dve_tokens(dve, 2)
                    dve_scores(dve, 0)
                    dve_features(dve, 1)
                    for i in range(LGROUP):
                        if i + 3 < LGROUP:
                            dve_tokens(dve, i + 3)
                        if i:
                            dve_out(dve, i - 1)
                        if i + 1 < LGROUP:
                            dve_scores(dve, i + 1)
                        if i:
                            dve_add(dve, i - 1)
                        if i + 2 < LGROUP:
                            dve_features(dve, i + 2)
                    dve_out(dve, LGROUP - 1)
                    dve_add(dve, LGROUP - 1)
            clear(nc, f.sems + list(s.values()))


def tail(nc, a, x, ident, minus_half, mv, bst, rstd, vare, banks, s_tail, s_mask):
    with ExitStack() as ctx:
        f = Tail(nc, ctx, x, ident, minus_half, mv, bst, rstd, vare)
        experts = Experts(nc, a, ctx)
        linear = Linear(nc, a, ctx)
        loads = experts.loads + linear.loads
        with nc.Block() as block:
            @block.sync
            def _(sp):
                for to, source in loads:
                    sp.dma_start(to, source).then_inc(s_tail, 16)
                sp.wait_ge(s_tail, 16 * len(loads))

            @block.gpsimd
            def _(pool):
                pool.memset(linear.head[:, :], 1.0).then_inc(s_mask, 1)
                pool.memset(linear.tri[:, :], 1.0).then_inc(s_mask, 1)
                pool.memset(linear.vx[:, :, :, :, :], 0.0).then_inc(s_mask, 1)
                pool.memset(linear.pick[:, :], 0.0).then_inc(s_mask, 1)
                pool.memset(linear.ones[:, :], 1.0).then_inc(s_mask, 1)
                pool.wait_ge(s_mask, 4)
                pool.memset(linear.own_columns(linear.pick[:, :]), 1.0).then_inc(s_mask, 1)
                pool.wait_ge(s_mask, 5)
                pool.affine_select(out=linear.tri[:, :], in_=linear.tri[:, :], compare_op=ALU.is_ge, fill=0.0, base=0,
                                   pattern=[[1, P]], channel_multiplier=-1).then_inc(s_mask, 1)
                pool.affine_select(out=linear.head[:, :], in_=linear.head[:, :], compare_op=ALU.is_ge, fill=0.0,
                                   base=0, pattern=[[-LD, LH]], channel_multiplier=1).then_inc(s_mask, 1)
                pool.wait_ge(s_mask, 8)
                pool.affine_select(out=linear.head[:, :], in_=linear.head[:, :], compare_op=ALU.is_ge, fill=0.0,
                                   base=LD - 1, pattern=[[LD, LH]], channel_multiplier=-1).then_inc(s_mask, 1)

            @block.vector
            def _(dve):
                dve.wait_ge(s_mask, 9)
                dve.tensor_reduce(linear.fourth[:, :],
                                  linear.head[:, :].rearrange("p (r m) -> p m r", m=ROWG), mybir.AxisListType.X,
                                  ALU.add)
                dve.wait_ge(s_tail, 16 * len(loads))
                dve.tensor_scalar(linear.nbg[:, :], linear.nbg[:, :], -1.0, None, ALU.mult)

        experts.run(nc, f, banks)
        linear.run(nc, f, banks)
        experts.run(nc, f, banks)


def kernel(**inputs):
    import numpy as _np
    import concourse.bacc as _bacc
    from concourse import mybir as _mybir
    from concourse.bass_utils import run_bass_kernel_spmd as _run

    given = {name[len("L0_"):]: _np.ascontiguousarray(value) for name, value in inputs.items()}
    names = {"x": "attn_a_x", "wq": "attn_a_wq", "wk": "attn_a_wk",
             "wv": "attn_a_wv", "mem_v": "attn_a_mem_v", "pre": "attn_a_pre_proj", "post": "attn_a_post_proj",
             "wo": "attn_a_wo", "bo": "attn_a_bo",
             "w1": "attn_a_w1", "w2": "attn_a_w2", "b2": "attn_a_b2",
             "ew1": "ffn_w1", "ew2": "ffn_w2", "eb2": "ffn_b2"}
    laid = {short: given[name] for short, name in names.items()}
    laid["gains"] = _np.ascontiguousarray(_np.stack(
        [given["attn_a_" + name] for name in ("ln1_g", "ln1_b", "ln2_g", "ln2_b")]).transpose(2, 0, 1))
    laid["b1"] = _np.ascontiguousarray(given["attn_a_b1"].reshape(DEPTH, FC, P).transpose(2, 0, 1))
    laid["router"] = _np.ascontiguousarray(given["ffn_router_w"].T)
    laid["eb1"] = _np.ascontiguousarray(given["ffn_b1"].reshape(EXPERTS, HC, P).transpose(2, 0, 1))
    for n in "qkgvo":
        laid["l" + n] = _np.ascontiguousarray(given["attn_b_W" + n].T)
    laid["lbg"] = given["attn_b_bg"].reshape(P, 1)
    laid["mem_kT"] = _np.ascontiguousarray(given["attn_a_mem_k"].transpose(0, 1, 3, 2))

    nc = _bacc.Bacc("TRN2", target_bir_lowering=False, num_devices=1)
    arrays, args = {}, {}
    for name, value in laid.items():
        arrays[f"in_{name}"] = value
        args[name] = nc.dram_tensor(f"in_{name}", value.shape, _mybir.dt.from_np(value.dtype), kind="ExternalInput").ap()
    out = nc.dram_tensor("out", (B, T, D), _mybir.dt.float32, kind="ExternalOutput").ap()
    program(nc, args, out)
    return _run(nc, [arrays], core_ids=[0]).results[0]["out"]
```
